# Optimizing a Trainium2 kernel written in Bass

```python
import numpy as np
import jax
import jax.numpy as jnp

def _softmax(x, axis=-1):
    return jax.nn.softmax(x, axis=axis)

def _gelu(x):
    return jax.nn.gelu(x, approximate=True)

def _silu(x):
    return jax.nn.silu(x)

def _sigmoid(x):
    return jax.nn.sigmoid(x)

def _layernorm(x, axis=-1, eps=1e-05):
    m = jnp.mean(x, axis=axis, keepdims=True)
    v = jnp.var(x, axis=axis, keepdims=True)
    return (x - m) / jnp.sqrt(v + eps)

def _scatter_add(tgt, idx, src, axis=0):
    return tgt.at[idx].add(src)

def _segment_sum(src, seg, n):
    return jax.ops.segment_sum(src, seg, n)
kernel_name = 'mk_adaln_attn_ffn_d1_seqx_r8_ee9bc7'

def setup_inputs(seed: int=0):
    np.random.seed(seed)
    _w = jnp.asarray

    def _rec_inputs():
        import jax
        import jax.numpy as jnp
        _rk = jax.random.key(seed)
        x = -0.000125 + 0.9999 * jax.random.normal(jax.random.fold_in(_rk, 1), (8, 128, 512), jnp.float32)
        _lenS = 128 - jax.random.randint(jax.random.fold_in(_rk, 7), (8,), 0, max(1, 128 // 4) + 1, jnp.int32)
        _lenS2 = 128 - jax.random.randint(jax.random.fold_in(_rk, 8), (8,), 0, max(1, 128 // 4) + 1, jnp.int32)
        condB_codebook = -0.0625 + 0.715345 * jax.random.normal(jax.random.fold_in(_rk, 11), (8,), jnp.float32)
        itok_B_0_7 = jax.random.randint(jax.random.fold_in(_rk, 12), (8,), 0, 8, jnp.int32)
        return (x, condB_codebook, itok_B_0_7)
    x, condB_codebook, itok_B_0_7 = _rec_inputs()

    def _L0_cond_setup():
        import jax, jax.numpy as jnp
        import numpy as np
        GROUP = 128
        LORA_ALPHA = 32.0
        LORA_RANK = 64
        key = jax.random.key(seed)
        k1, k2, k3, k4 = jax.random.split(key, 4)
        O, I = (512, 512)
        x = jax.random.normal(k1, (4, 256, I), dtype=jnp.float32)
        weight = jax.random.normal(k2, (O, I), dtype=jnp.float32) * 0.02
        wg = weight.reshape(O, I // GROUP, GROUP)
        scale_log = jnp.log(jnp.clip(jnp.max(jnp.abs(wg), axis=2, keepdims=True), 1e-05))
        codebook = jnp.array([-1.0, -0.25, 0.0, 1.0], dtype=jnp.float32)
        lora_A = jax.random.normal(k3, (LORA_RANK, I), dtype=jnp.float32) * 0.02
        lora_B = jax.random.normal(k4, (O, LORA_RANK), dtype=jnp.float32) * 0.02
        return {'x': x, 'weight': weight, 'scale_log': scale_log, 'codebook': codebook, 'lora_A': lora_A, 'lora_B': lora_B}
    _L0_cond_all = _L0_cond_setup()
    _L0_cond_in = {k: v for k, v in _L0_cond_all.items() if k in ('weight', 'scale_log', 'lora_A', 'lora_B')}
    del _L0_cond_all

    def _L0_attn_setup():
        import jax, jax.numpy as jnp
        import numpy as np
        H = 512
        D = H // 4
        key = jax.random.key(seed)
        k1, k2, k3, k4, k5 = jax.random.split(key, 5)
        x = jax.random.normal(k1, (4, 512, H), dtype=jnp.float32)
        s_in = 1.0 / np.sqrt(H)
        Wqkv = jax.random.normal(k2, (H, 3 * D), dtype=jnp.float32) * s_in
        bqkv = jax.random.normal(k3, (3 * D,), dtype=jnp.float32) * 0.01
        Wo = jax.random.normal(k4, (D, H), dtype=jnp.float32) * (1.0 / np.sqrt(D))
        bo = jax.random.normal(k5, (H,), dtype=jnp.float32) * 0.01
        return {'x': x, 'Wqkv': Wqkv, 'bqkv': bqkv, 'Wo': Wo, 'bo': bo}
    _L0_attn_all = _L0_attn_setup()
    _L0_attn_in = {k: v for k, v in _L0_attn_all.items() if k in ('Wqkv', 'bqkv', 'Wo', 'bo')}
    del _L0_attn_all

    def _L0_cond2_setup():
        import jax, jax.numpy as jnp
        import numpy as np
        TOP_K = 2
        LANG_BIAS = 5.0
        SCALING = 32.0 / 16.0
        LANGUAGE_PAD_ID = -1
        key = jax.random.key(seed)
        ks = jax.random.split(key, 6)
        B, T, D, O, E, R = (4, 256, 512, 512, 8, 16)
        x = jax.random.normal(ks[0], (B, T, D), dtype=jnp.float32)
        language_ids = jax.random.randint(ks[1], (B,), 0, E).astype(jnp.int64)
        W = jax.random.normal(ks[2], (O, D), dtype=jnp.float32) * (1.0 / np.sqrt(D))
        Wr = jax.random.normal(ks[3], (E, D), dtype=jnp.float32) * (1.0 / np.sqrt(D))
        A = jax.random.normal(ks[4], (E, R, D), dtype=jnp.float32) * (1.0 / np.sqrt(D))
        Bm = jax.random.normal(ks[5], (O, R), dtype=jnp.float32) * 0.0
        Bm = jnp.broadcast_to(Bm, (E, O, R)) + jax.random.normal(ks[5], (E, O, R), dtype=jnp.float32) * 0.02
        return {'x': x, 'language_ids': language_ids, 'W': W, 'Wr': Wr, 'A': A, 'B': Bm}
    _L0_cond2_all = _L0_cond2_setup()
    _L0_cond2_in = {k: v for k, v in _L0_cond2_all.items() if k in ('W', 'Wr', 'A', 'B')}
    del _L0_cond2_all

    def _L0_ffn_setup():
        import jax, jax.numpy as jnp
        import numpy as np
        OUT, IN = (512, 512)
        B, S = (4, 256)

        def _quantize(w):
            min_val, max_val = (jnp.min(w), jnp.max(w))
            scale = (max_val - min_val) / 255.0
            zp = 255.0 - max_val / scale
            zp = jnp.clip(zp, 0.0, 255.0)
            zp = jnp.round(zp)
            q = jnp.round(jnp.clip(zp + w / scale, 0.0, 255.0)).astype(jnp.int32)
            return (q, scale, zp)
        key = jax.random.key(seed)
        kx, kw, kb = jax.random.split(key, 3)
        x = jax.random.normal(kx, (B, S, IN), dtype=jnp.float32)
        w_fp = jax.random.normal(kw, (OUT, IN), dtype=jnp.float32) * 0.02
        bias = jax.random.normal(kb, (OUT,), dtype=jnp.float32) * 0.01
        qweight, scale, zero_point = _quantize(w_fp)
        return {'x': x, 'qweight': qweight, 'scale': scale, 'zero_point': zero_point, 'bias': bias}
    _L0_ffn_all = _L0_ffn_setup()
    _L0_ffn_in = {k: v for k, v in _L0_ffn_all.items() if k in ('qweight', 'scale', 'zero_point', 'bias')}
    del _L0_ffn_all
    return {'x': x, 'condB_codebook': condB_codebook, 'itok_B_0_7': itok_B_0_7, 'L0_cond_weight': _L0_cond_in['weight'], 'L0_cond_scale_log': _L0_cond_in['scale_log'], 'L0_cond_lora_A': _L0_cond_in['lora_A'], 'L0_cond_lora_B': _L0_cond_in['lora_B'], 'L0_attn_Wqkv': _L0_attn_in['Wqkv'], 'L0_attn_bqkv': _L0_attn_in['bqkv'], 'L0_attn_Wo': _L0_attn_in['Wo'], 'L0_attn_bo': _L0_attn_in['bo'], 'L0_cond2_W': _L0_cond2_in['W'], 'L0_cond2_Wr': _L0_cond2_in['Wr'], 'L0_cond2_A': _L0_cond2_in['A'], 'L0_cond2_B': _L0_cond2_in['B'], 'L0_ffn_qweight': _L0_ffn_in['qweight'], 'L0_ffn_scale': _L0_ffn_in['scale'], 'L0_ffn_zero_point': _L0_ffn_in['zero_point'], 'L0_ffn_bias': _L0_ffn_in['bias']}

def reference(x, condB_codebook, itok_B_0_7, L0_cond_weight, L0_cond_scale_log, L0_cond_lora_A, L0_cond_lora_B, L0_attn_Wqkv, L0_attn_bqkv, L0_attn_Wo, L0_attn_bo, L0_cond2_W, L0_cond2_Wr, L0_cond2_A, L0_cond2_B, L0_ffn_qweight, L0_ffn_scale, L0_ffn_zero_point, L0_ffn_bias):
    import jax
    import jax.numpy as jnp

    def _L0_cond_ref(x, weight, scale_log, codebook, lora_A, lora_B):
        import jax, jax.numpy as jnp
        import numpy as np
        GROUP = 128
        LORA_ALPHA = 32.0
        LORA_RANK = 64
        O, I = weight.shape
        lora_delta = lora_B @ lora_A * (LORA_ALPHA / LORA_RANK)
        cb = codebook / jnp.clip(jnp.max(jnp.abs(codebook)), 1e-08)
        scale = jnp.exp(scale_log)
        wg = (weight + lora_delta).reshape(O, I // GROUP, GROUP)
        normalized = wg / scale
        thresholds = (cb[:-1] + cb[1:]) * 0.5
        idx = jnp.searchsorted(thresholds, normalized, side='left')
        quantized = cb[idx]
        w = jax.lax.stop_gradient(quantized - normalized) + normalized
        w_q = (w * scale).reshape(O, I)
        w_eff = w_q + lora_delta
        return x @ w_eff.T

    def _L0_attn_ref(x, Wqkv, bqkv, Wo, bo):
        import jax, jax.numpy as jnp
        import numpy as np
        H = 512
        D = H // 4
        B, S, C = x.shape
        d = C // 4
        qkv = jnp.einsum('bsc,cf->bsf', x, Wqkv) + bqkv
        qkv = qkv.reshape(B, S, 3, d)
        q, k, v = (qkv[:, :, 0], qkv[:, :, 1], qkv[:, :, 2])
        scale = 1.0 / jnp.sqrt(jnp.float32(d)).astype(x.dtype)
        attn = jnp.einsum('bqd,bkd->bqk', q, k) * scale
        attn = jax.nn.softmax(attn, axis=-1)
        out = jnp.einsum('bqk,bkd->bqd', attn, v)
        return jnp.einsum('bqd,dc->bqc', out, Wo) + bo

    def _L0_cond2_ref(x, language_ids, W, Wr, A, B):
        import jax, jax.numpy as jnp
        import numpy as np
        TOP_K = 2
        LANG_BIAS = 5.0
        SCALING = 32.0 / 16.0
        LANGUAGE_PAD_ID = -1
        base = jnp.einsum('btd,od->bto', x, W)
        E = Wr.shape[0]
        logits = jnp.einsum('btd,ed->bte', x.astype(jnp.float32), Wr.astype(jnp.float32))
        expert_targets = language_ids
        valid = expert_targets >= 0
        tgt = jnp.where(valid, expert_targets, 0)
        bias = jax.nn.one_hot(tgt, E, dtype=logits.dtype) * LANG_BIAS
        bias = jnp.where(valid[:, None], bias, 0.0)
        logits = logits + bias[:, None, :]
        topw, topi = jax.lax.top_k(logits, TOP_K)
        weights = jax.nn.softmax(topw, axis=-1)
        gates = jnp.sum(jax.nn.one_hot(topi, E, dtype=weights.dtype) * weights[..., None], axis=-2)
        gates = gates.astype(x.dtype)
        h = jnp.einsum('btd,erd->bter', x, A)
        lora_out = jnp.einsum('bter,bte,eor->bto', h, gates, B)
        return base + SCALING * lora_out

    def _L0_ffn_ref(x, qweight, scale, zero_point, bias):
        import jax, jax.numpy as jnp
        import numpy as np
        OUT, IN = (512, 512)
        B, S = (4, 256)

        def _quantize(w):
            min_val, max_val = (jnp.min(w), jnp.max(w))
            scale = (max_val - min_val) / 255.0
            zp = 255.0 - max_val / scale
            zp = jnp.clip(zp, 0.0, 255.0)
            zp = jnp.round(zp)
            q = jnp.round(jnp.clip(zp + w / scale, 0.0, 255.0)).astype(jnp.int32)
            return (q, scale, zp)
        w = scale * (qweight.astype(x.dtype) - zero_point)
        return jnp.einsum('bsi,oi->bso', x, w) + bias
    x = x + _L0_attn_ref(_L0_cond_ref(x, L0_cond_weight, L0_cond_scale_log, condB_codebook, L0_cond_lora_A, L0_cond_lora_B), L0_attn_Wqkv, L0_attn_bqkv, L0_attn_Wo, L0_attn_bo)
    x = x + _L0_ffn_ref(_L0_cond2_ref(x, itok_B_0_7, L0_cond2_W, L0_cond2_Wr, L0_cond2_A, L0_cond2_B), L0_ffn_qweight, L0_ffn_scale, L0_ffn_zero_point, L0_ffn_bias)
    return x

_drawn_inputs = setup_inputs


def setup_inputs(seed=0):
    import zlib

    import numpy as np

    out = dict(_drawn_inputs(seed))
    spreads = {}
    factors = {'L0_cond_lora_A': 3.056,
     'L0_cond_lora_B': 2.933,
     'L0_attn_bqkv': 5.153,
     'L0_attn_bo': 5.871,
     'L0_cond2_Wr': 8.0,
     'L0_ffn_bias': 6.264}
    for name, (base, spread) in spreads.items():
        noise = np.random.default_rng([zlib.crc32(name.encode()), seed]).standard_normal(out[name].shape)
        drawn = base * np.exp(spread * noise) if base else spread * noise
        out[name] = jnp.asarray(drawn.astype(out[name].dtype))
    for name, factor in factors.items():
        out[name] = (out[name] * factor).astype(out[name].dtype)
    return out
```

```python
from contextlib import ExitStack

import concourse.bass as bass
from concourse import mybir

F32 = mybir.dt.float32
F32R = mybir.dt.float32r
I32 = mybir.dt.int32
U32 = mybir.dt.uint32
ALU = mybir.AluOpType
ACT = mybir.ActivationFunctionType
AX = mybir.AxisListType

P = 128


def block_kernel(nc, x, codebook, lang, cond_w, scale_log, lora_a, lora_b, wqkv, bqkv, wo, bo,
                 moe_w, router, exp_a, exp_b, qweight, ffn_scale, zero_point, ffn_bias, out):
    BATCH, SEQ, C = x.shape
    CT = C // P
    HALVES = 2
    TPH = BATCH // HALVES
    HT = TPH * SEQ
    D = wo.shape[0]
    RANK = lora_a.shape[0]
    E, R, _ = exp_a.shape
    ER = E * R
    HL = ER + E
    LEVELS = codebook.shape[0]
    CUTS = LEVELS - 1
    SOFTMAX_SCALE = float(D) ** -0.5
    LORA_SCALE = 32.0 / 64.0
    LANG_BIAS = 5.0
    EXPERT_SCALE = 32.0 / 16.0
    CODEBOOK_FLOOR = 1e-8
    assert SEQ == P and D == P and ER == P and 2 * RANK == P and HT == 512 and C == 512
    assert LEVELS == 8 and E == 8

    with ExitStack() as ctx:
        def sb(name, shape, dt=F32):
            return ctx.enter_context(nc.sbuf_tensor(name, shape, dt))

        def sem(name):
            return ctx.enter_context(nc.semaphore(name))

        x_nat = sb("x_nat", [P, BATCH, C])
        cond_n = sb("cond_n", [P, HALVES, 2 * C])
        q_nat = sb("q_nat", [P, CT, C])
        moe_nat = sb("moe_nat", [P, CT, C])
        wqkv_nat = sb("wqkv_nat", [P, CT, 3 * D])
        expa_nat = sb("expa_nat", [P, C])
        router_nat = sb("router_nat", [E, C])
        wo_nat = sb("wo_nat", [D, C])
        expb_nat = sb("expb_nat", [P, CT, E, R])
        lora_b_dup = sb("lora_b_dup", [P, CT, 2, RANK])
        lora_a_dup = sb("lora_a_dup", [P, C])
        scale = sb("scale", [P, CT * CT])
        inv_scale = sb("inv_scale", [P, CT * CT])
        ffn_bias_bc = sb("ffn_bias_bc", [P, C])
        bias_rows = sb("bias_rows", [3 + CT, P])
        bias_cols = sb("bias_cols", [P, 3 + CT])
        qkv_bias, bo_col = bias_cols[:, 0:3], bias_cols[:, 3:3 + CT]
        ffn_scal = sb("ffn_scal", [P, 3])
        lang_i = sb("lang_i", [P, BATCH], I32)
        cb = sb("cb", [P, LEVELS])
        cb_tmp = sb("cb_tmp", [P, 4])
        cuts = sb("cuts", [P, CUTS])
        rises = sb("rises", [P, CUTS])
        ident = sb("ident", [P, P])
        xT = sb("xT", [P, CT, BATCH * SEQ])
        xT_hi = sb("xT_hi", [P, CT, BATCH * SEQ], F32R)
        xT_lo = sb("xT_lo", [P, CT, BATCH * SEQ], F32R)
        lora_bT = sb("lora_bT", [P, C], F32R)
        lora_bT_tmp = sb("lora_bT_tmp", [P, C], F32R)
        lora_a_hi = sb("lora_a_hi", [P, C], F32R)
        lora_a_lo = sb("lora_a_lo", [P, C], F32R)
        split_a_hi = sb("split_a_hi", [P, CT, C], F32R)
        split_a_lo = sb("split_a_lo", [P, CT, C], F32R)
        split_b_hi = sb("split_b_hi", [P, CT, C], F32R)
        split_b_lo = sb("split_b_lo", [P, CT, C], F32R)
        G_hi = sb("G_hi", [P, CT, C], F32R)
        G_lo = sb("G_lo", [P, CT, C], F32R)
        wqkv_hi = sb("wqkv_hi", [P, CT, 3 * D], F32R)
        wqkv_lo = sb("wqkv_lo", [P, CT, 3 * D], F32R)
        expb_hi = sb("expb_hi", [P, CT, ER], F32R)
        expb_lo = sb("expb_lo", [P, CT, ER], F32R)
        Bf = expa_nat
        Bf_hi = sb("Bf_hi", [P, C], F32R)
        Bf_lo = sb("Bf_lo", [P, C], F32R)
        hlT = sb("hlT", [P, CT, HL])
        woT = sb("woT", [P, CT, D])
        woT_hi = lora_bT[:, :].rearrange("p (t n) -> p t n", t=CT)
        woT_lo = lora_bT_tmp[:, :].rearrange("p (t n) -> p t n", t=CT)
        boR = wo_nat[:, :].rearrange("p (t n) -> p t n", t=CT)
        boR_hi = lora_a_hi[:, :].rearrange("p (t n) -> p t n", t=CT)
        boR_lo = lora_a_lo[:, :].rearrange("p (t n) -> p t n", t=CT)
        woG_hi = expb_hi[:, :, :].rearrange("p t n -> p (t n)")
        woG_lo = expb_lo[:, :, :].rearrange("p t n -> p (t n)")
        woHL = sb("woHL", [D, HL])
        y_bias = ffn_bias_bc
        hl_bias = sb("hl_bias", [P, HL])
        delta = sb("delta", [P, HALVES, 2 * C])
        acc = x_nat[:, :, :].rearrange("p (k t) c -> p k (t c)", k=4)
        step = q_nat[:, :, :].rearrange("p (h t) n -> p h (t n)", h=HALVES)

        def place(ap, n):
            return ap[:, 2 * n:2 * n + 2, :]

        def row(ap, n):
            return ap[:, n, :].rearrange("p (h t) -> p h t", h=HALVES)

        qT, kT = row(cond_n, 0), row(cond_n, 1)
        vT, v = row(delta, 0), row(delta, 1)
        probs, probsT = place(moe_nat, 0), place(moe_nat, 1)
        oT, gh = place(q_nat, 0), place(q_nat, 1)
        oT_hi, ghT_hi = place(split_a_hi, 0), place(split_a_hi, 1)
        oT_lo, ghT_lo = place(split_a_lo, 0), place(split_a_lo, 1)
        neg_max = sb("neg_max", [P, BATCH])
        row_sum = sb("row_sum", [P, BATCH])
        hl = sb("hl", [P, BATCH, HL])
        lang_f = sb("lang_f", [P, BATCH])
        lang_hot = sb("lang_hot", [P, BATCH, E])
        expert_no = sb("expert_no", [P, E])
        top = sb("top", [P, BATCH, 8])
        top_at = sb("top_at", [P, BATCH, 8], U32)
        top_exp = sb("top_exp", [P, BATCH])
        w_first = sb("w_first", [P, BATCH])
        w_second = sb("w_second", [P, BATCH])
        gate = sb("gate", [P, BATCH, E])
        gate2 = sb("gate2", [P, BATCH, E])
        y_out = x_nat

        psum = [ctx.enter_context(nc.psum_tensor(f"psum{b}", [P, 512], F32)) for b in range(8)]

        LOADS = ["lora_b", "lora_a", "codebook", "scale_log", "cond_w0", "cond_w1", "x0", "x1",
                 "qweight", "ffn_scal", "moe_w", "exp_a", "router", "wo", "exp_b", "wqkv", "biases",
                 "ffn_bias", "lang"]
        loaded = {n: sem(f"ld_{n}") for n in LOADS}
        lora_bT_done = sem("lora_bT_done")
        xT_done = sem("xT_done")
        delta_done = sem("delta_done")
        hlT_done = sem("hlT_done")
        dT_done = sem("dT_done")
        woT_done = sem("woT_done")
        G_done = sem("G_done")
        Bf_done = sem("Bf_done")
        woG_done = sem("woG_done")
        woHL_done = sem("woHL_done")
        boG_done = sem("boG_done")
        xhl_done = sem("xhl_done")
        M_done = sem("M_done")
        qkvT_done = sem("qkvT_done")
        v_done = sem("v_done")
        scores_done = sem("scores_done")
        probsT_done = sem("probsT_done")
        oT_done = sem("oT_done")
        hl_done = sem("hl_done")
        ghT_done = sem("ghT_done")
        y_done = sem("y_done")
        scale_ready = sem("scale_ready")
        lora_bT_hi_ready = sem("lora_bT_hi_ready")
        lora_a_hi_ready = sem("lora_a_hi_ready")
        xT_ready = sem("xT_ready")
        delta_ready = sem("delta_ready")
        hlT_ready = sem("hlT_ready")
        dT_hi_ready = sem("dT_hi_ready")
        woT_ready = sem("woT_ready")
        G_ready = sem("G_ready")
        G_hi_ready = sem("G_hi_ready")
        Bf_ready = sem("Bf_ready")
        woG_hi_ready = sem("woG_hi_ready")
        woHL_ready = sem("woHL_ready")
        w_eff_hi_ready = sem("w_eff_hi_ready")
        M_hi_ready = sem("M_hi_ready")
        qkvT_ready = sem("qkvT_ready")
        v_ready = sem("v_ready")
        exp_ready = sem("exp_ready")
        probsT_ready = sem("probsT_ready")
        oT_ready = sem("oT_ready")
        oT_hi_ready = sem("oT_hi_ready")
        top_exp_ready = sem("top_exp_ready")
        ghT_hi_ready = sem("ghT_hi_ready")
        dve_step = sem("dve_step")
        lora_bT_ready = sem("lora_bT_ready")
        qmz_ready = sem("qmz_ready")
        dT_lo_ready = sem("dT_lo_ready")
        xT_hi_ready = sem("xT_hi_ready")
        woT_hi_ready = sem("woT_hi_ready")
        woT_lo_ready = sem("woT_lo_ready")
        Bf_lo_ready = sem("Bf_lo_ready")
        boR_ready = sem("boR_ready")
        woG_lo_ready = sem("woG_lo_ready")
        y_bias_ready = sem("y_bias_ready")
        hl_x_ready = sem("hl_x_ready")
        scal_ready = sem("scal_ready")
        w_eff_ready = sem("w_eff_ready")
        M_lo_ready = sem("M_lo_ready")
        max_ready = sem("max_ready")
        probs_ready = sem("probs_ready")
        oT_lo_ready = sem("oT_lo_ready")
        hl_read = sem("hl_read")
        top_diff_ready = sem("top_diff_ready")
        gh_ready = sem("gh_ready")
        ghT_lo_ready = sem("ghT_lo_ready")
        y_ready = sem("y_ready")
        pool_step = sem("pool_step")
        ident_ready = sem("ident_ready")
        lora_a_lo_ready = sem("lora_a_lo_ready")
        moe_split_ready = sem("moe_split_ready")
        expb_ready = sem("expb_ready")
        G_sum_ready = sem("G_sum_ready")
        G_lo_ready = sem("G_lo_ready")
        xT_lo_ready = sem("xT_lo_ready")
        wqkv_ready = sem("wqkv_ready")
        w_eff_lo_ready = sem("w_eff_lo_ready")
        stored = sem("stored")

        block = ctx.enter_context(nc.Block())

        @block.sync
        def _(sp):
            def load(name, dst, src):
                sp.dma_start(dst, src).then_inc(loaded[name], 16)

            rows = "(t p) n -> p t n"
            lb = lora_b.rearrange(rows, p=P)
            load("lora_b", lora_b_dup[:, :, 0, :], lb)
            load("lora_b", lora_b_dup[:, :, 1, :], lb)
            load("lora_a", lora_a_dup[0:RANK, :], lora_a)
            load("lora_a", lora_a_dup[RANK:P, :], lora_a)
            load("codebook", cb[:, :], codebook.partition_broadcast(P))
            load("scale_log", scale[:, :].rearrange("p (t g) -> p t g", t=CT), scale_log.rearrange("(t p) g -> p t g", p=P))
            cw = cond_w.rearrange(rows, p=P)
            for h in range(HALVES):
                load(f"cond_w{h}", cond_n[:, h, :].rearrange("p (t n) -> p t n", t=2), cw[:, 2 * h:2 * h + 2, :])
            load("ffn_scal", ffn_scal[:, 0:1], ffn_scale.partition_broadcast(P))
            load("ffn_scal", ffn_scal[:, 1:2], zero_point.partition_broadcast(P))
            load("qweight", q_nat[:, :, :].bitcast(I32), qweight.rearrange(rows, p=P))
            load("moe_w", moe_nat[:, :, :], moe_w.rearrange(rows, p=P))
            for t in range(CT):
                load("exp_b", expb_nat[:, t, :, :], exp_b[:, t * P:(t + 1) * P, :].rearrange("e p r -> p e r"))
            load("x1", x_nat[:, TPH:BATCH, :], x[TPH:BATCH].rearrange("b p c -> p b c"))
            load("wqkv", wqkv_nat[:, :, :], wqkv.rearrange(rows, p=P))
            load("ffn_bias", ffn_bias_bc[:, :], ffn_bias.partition_broadcast(P))
            for b in range(BATCH):
                sp.wait_ge(y_ready, b + 1)
                sp.dma_start(out[b], y_out[:, b, :]).then_inc(stored, 16)
            sp.wait_ge(stored, 16 * BATCH)

        @block.scalar
        def _(act):
            def load(name, dst, src):
                act.dma_start(dst, src).then_inc(loaded[name], 16)

            load("x0", x_nat[:, 0:TPH, :], x[0:TPH].rearrange("b p c -> p b c"))
            load("exp_a", expa_nat[:, :], exp_a.rearrange("e r c -> (e r) c"))
            load("router", router_nat[:, :], router)
            load("wo", wo_nat[:, :], wo)
            load("biases", bias_rows[0:3, :], bqkv.rearrange("(j p) -> j p", p=P))
            load("biases", bias_rows[3:3 + CT, :], bo.rearrange("(t p) -> t p", p=P))
            load("lang", lang_i[:, :], lang.partition_broadcast(P))

            act.wait_ge(loaded["scale_log"], 16)
            act.activation(scale[:, :], scale[:, :], ACT.Exp).then_inc(scale_ready, 1)
            act.wait_ge(loaded["lora_a"], 32)
            act.activation(lora_a_hi[:, :], lora_a_dup[:, :], ACT.Copy).then_inc(lora_a_hi_ready, 1)
            act.wait_ge(lora_bT_done, 1)
            act.activation(lora_bT[0:RANK, :], psum[0][0:RANK, :], ACT.Copy).then_inc(lora_bT_hi_ready, 1)
            act.activation(lora_bT_tmp[RANK:P, :], psum[0][RANK:P, :], ACT.Copy).then_inc(lora_bT_hi_ready, 1)

            def x_out(h, banks):
                for c in range(CT):
                    act.wait_ge(xT_done, CT * h + c + 1)
                    act.activation(xT[:, c, h * HT:(h + 1) * HT], psum[banks[c]][:, :], ACT.Copy)\
                       .then_inc(xT_ready, 1)

            x_out(0, (1, 2, 3, 4))
            for o, b in enumerate((5, 6, 7, 0)):
                act.wait_ge(delta_done, o + 1)
                act.activation(delta[:, o // 2, (o % 2) * C:(o % 2 + 1) * C], psum[b][:, :], ACT.Copy,
                               scale=LORA_SCALE).then_inc(delta_ready, 1)
            for o in range(CT):
                act.wait_ge(dT_done, o + 1)
                act.activation(split_b_hi[:, o, :], psum[1 + o][:, :], ACT.Copy).then_inc(dT_hi_ready, 1)
            act.wait_ge(hlT_done, 1)
            act.activation(hlT[:, :, 0:ER], psum[5][:, :].rearrange("p (t n) -> p t n", t=CT), ACT.Copy)\
               .then_inc(hlT_ready, 1)
            act.wait_ge(hlT_done, 2)
            act.activation(hlT[:, :, ER:HL], psum[6][:, 0:CT * E].rearrange("p (t n) -> p t n", t=CT), ACT.Copy)\
               .then_inc(hlT_ready, 1)
            act.activation(bias_cols[:, :], psum[6][:, CT * E:CT * E + 3 + CT], ACT.Copy).then_inc(hlT_ready, 1)
            act.wait_ge(woT_done, 1)
            act.activation(woT[:, :, :], psum[7][:, :].rearrange("p (t n) -> p t n", t=CT), ACT.Copy)\
               .then_inc(woT_ready, 1)
            x_out(1, (0, 5, 6, 7))

            for i in range(CT):
                act.wait_ge(G_done, i + 1)
                if i == 0:
                    act.wait_ge(loaded["ffn_scal"], 32)
                    act.wait_ge(moe_split_ready, CT)
                act.activation(moe_nat[:, i, :], psum[1 + i][:, :], ACT.Copy, scale=ffn_scal[:, 0:1])\
                   .then_inc(G_ready, 1)
                if i >= 1:
                    act.wait_ge(G_sum_ready, i)
                    act.activation(G_hi[:, i - 1, :], moe_nat[:, i - 1, :], ACT.Copy).then_inc(G_hi_ready, 1)
            act.wait_ge(G_sum_ready, CT)
            act.activation(G_hi[:, CT - 1, :], moe_nat[:, CT - 1, :], ACT.Copy).then_inc(G_hi_ready, 1)
            act.wait_ge(Bf_done, 1)
            act.wait_ge(scal_ready, 1)
            act.activation(Bf[:, :], psum[0][:, :], ACT.Copy, scale=ffn_scal[:, 2:3]).then_inc(Bf_ready, 1)
            act.wait_ge(woHL_done, 1)
            act.activation(woHL[:, :], psum[6][:, 0:HL], ACT.Copy).then_inc(woHL_ready, 1)
            act.wait_ge(woHL_done, 2)
            act.activation(hl_bias[:, :], psum[6][:, 256:256 + HL], ACT.Copy).then_inc(woHL_ready, 1)
            act.wait_ge(woG_done, 1)
            act.activation(woG_hi[:, :], psum[5][:, :], ACT.Copy).then_inc(woG_hi_ready, 1)

            for h in range(HALVES):
                act.wait_ge(w_eff_ready, h + 1)
                act.activation(split_a_hi[:, 2 * h:2 * h + 2, :].rearrange("p t n -> p (t n)"), acc[:, h, :],
                               ACT.Copy).then_inc(w_eff_hi_ready, 1)
            for i in range(CT):
                act.wait_ge(M_done, i + 1)
                act.activation(split_b_hi[:, i, 0:3 * D], psum[i][:, 0:3 * D], ACT.Copy).then_inc(M_hi_ready, 1)

            def qkv_out(h, which, bank, n):
                act.wait_ge(qkvT_done, n)
                if which == 2:
                    act.activation(vT[:, h, :], psum[bank][:, :], ACT.Copy).then_inc(qkvT_ready, 1)
                else:
                    act.activation((qT, kT)[which][:, h, :], psum[bank][:, :], ACT.Identity,
                                   bias=qkv_bias[:, which:which + 1]).then_inc(qkvT_ready, 1)

            def v_out(h, bank):
                act.wait_ge(v_done, h + 1)
                act.activation(v[:, h, :], psum[bank][:, :], ACT.Copy).then_inc(v_ready, 1)

            def exps(h, bank):
                act.wait_ge(max_ready, h + 1)
                for b in range(TPH):
                    n = TPH * h + b
                    act.activation(probs[:, h, b * P:(b + 1) * P], psum[bank][:, b * P:(b + 1) * P], ACT.Exp,
                                   bias=neg_max[:, n:n + 1], scale=SOFTMAX_SCALE,
                                   accum_out=row_sum[:, n:n + 1]).then_inc(exp_ready, 1)

            def probsT_out(h, bank):
                act.wait_ge(probsT_done, h + 1)
                act.activation(probsT[:, h, :], psum[bank][:, :], ACT.Copy).then_inc(probsT_ready, 1)

            def oT_out(h, bank):
                act.wait_ge(oT_done, h + 1)
                act.activation(oT[:, h, :], psum[bank][:, :], ACT.Identity, bias=qkv_bias[:, 2:3])\
                   .then_inc(oT_ready, 1)
                act.wait_ge(oT_ready, h + 1)
                act.activation(oT_hi[:, h, :], oT[:, h, :], ACT.Copy).then_inc(oT_hi_ready, 1)

            def top_exps(h):
                act.wait_ge(top_diff_ready, h + 1)
                act.activation(top_exp[:, TPH * h:TPH * (h + 1)], top_exp[:, TPH * h:TPH * (h + 1)], ACT.Exp)\
                   .then_inc(top_exp_ready, 1)

            def ghT_out(h, bank):
                act.wait_ge(ghT_done, h + 1)
                act.activation(ghT_hi[:, h, :], psum[bank][:, :], ACT.Copy).then_inc(ghT_hi_ready, 1)

            act.wait_ge(hlT_ready, 3)
            qkv_out(0, 2, 0, 1)
            qkv_out(0, 0, 1, 2)
            qkv_out(0, 1, 2, 3)
            v_out(0, 3)
            exps(0, 0)
            qkv_out(1, 2, 1, 4)
            v_out(1, 2)
            probsT_out(0, 3)
            qkv_out(1, 0, 0, 5)
            oT_out(0, 1)
            qkv_out(1, 1, 2, 6)
            top_exps(0)
            exps(1, 1)
            ghT_out(0, 0)
            probsT_out(1, 1)
            oT_out(1, 2)
            top_exps(1)
            ghT_out(1, 1)

        @block.gpsimd
        def _(pool):
            steps = [0]

            def alone(ins):
                steps[0] += 1
                ins.then_inc(pool_step, 1)
                pool.wait_ge(pool_step, steps[0])

            alone(pool.memset(ident[:, :], 0.0))
            pool.affine_select(out=ident[:, :], in_=ident[:, :], compare_op=ALU.not_equal, fill=1.0,
                               base=0, pattern=[[-1, P]], channel_multiplier=1).then_inc(ident_ready, 1)
            for e in range(E):
                pool.memset(expert_no[:, e:e + 1], float(e)).then_inc(ident_ready, 1)
            pool.wait_ge(lora_a_hi_ready, 1)
            pool.tensor_tensor(lora_a_lo[:, :], lora_a_dup[:, :], lora_a_hi[:, :], ALU.subtract)\
                .then_inc(lora_a_lo_ready, 1)

            def split(full, hi, lo, ready):
                alone(pool.tensor_scalar(hi, full, 1.0, 0.0, ALU.mult, ALU.add))
                pool.tensor_tensor(lo, full, hi, ALU.subtract).then_inc(ready, 1)

            pool.wait_ge(loaded["moe_w"], 16)
            for o in range(CT):
                split(moe_nat[:, o, :], split_a_hi[:, o, :], split_a_lo[:, o, :], moe_split_ready)
            pool.wait_ge(loaded["exp_b"], 16 * CT)
            split(expb_nat[:, :, :, :].rearrange("p t e r -> p (t e r)"), expb_hi[:, :, :].rearrange("p t n -> p (t n)"),
                  expb_lo[:, :, :].rearrange("p t n -> p (t n)"), expb_ready)

            def x_lo(h):
                pool.wait_ge(xT_hi_ready, h + 1)
                s = slice(h * HT, (h + 1) * HT)
                for c in range(CT):
                    pool.tensor_tensor(xT_lo[:, c, s], xT[:, c, s], xT_hi[:, c, s], ALU.subtract)\
                        .then_inc(xT_lo_ready, 1)

            x_lo(0)
            for i in range(CT):
                pool.wait_ge(G_ready, i + 1)
                d = moe_nat[:, i, i * P:(i + 1) * P]
                pool.tensor_tensor(d, d, ident[:, :], ALU.add).then_inc(G_sum_ready, 1)
                if i >= 1:
                    pool.wait_ge(G_hi_ready, i)
                    pool.tensor_tensor(G_lo[:, i - 1, :], moe_nat[:, i - 1, :], G_hi[:, i - 1, :], ALU.subtract)\
                        .then_inc(G_lo_ready, 1)
            pool.wait_ge(G_hi_ready, CT)
            pool.tensor_tensor(G_lo[:, CT - 1, :], moe_nat[:, CT - 1, :], G_hi[:, CT - 1, :], ALU.subtract)\
                .then_inc(G_lo_ready, 1)
            pool.wait_ge(loaded["wqkv"], 16)
            for o in range(CT):
                split(wqkv_nat[:, o, :], wqkv_hi[:, o, :], wqkv_lo[:, o, :], wqkv_ready)
            for h in range(HALVES):
                pool.wait_ge(w_eff_hi_ready, h + 1)
                s = slice(2 * h, 2 * h + 2)
                pool.tensor_tensor(split_a_lo[:, s, :].rearrange("p t n -> p (t n)"), acc[:, h, :],
                                   split_a_hi[:, s, :].rearrange("p t n -> p (t n)"), ALU.subtract)\
                    .then_inc(w_eff_lo_ready, 1)
            x_lo(1)

        @block.vector
        def _(dve):
            steps = [0]

            def mark(ins):
                steps[0] += 1
                ins.then_inc(dve_step, 1)
                return steps[0]

            def alone(ins):
                dve.wait_ge(dve_step, mark(ins))

            dve.wait_ge(loaded["codebook"], 16)
            alone(dve.tensor_reduce(cb_tmp[:, 0:1], cb[:, :], AX.X, ALU.max))
            alone(dve.tensor_reduce(cb_tmp[:, 1:2], cb[:, :], AX.X, ALU.min))
            alone(dve.tensor_scalar(cb_tmp[:, 1:2], cb_tmp[:, 1:2], -1.0, CODEBOOK_FLOOR, ALU.mult, ALU.max))
            alone(dve.tensor_tensor(cb_tmp[:, 2:3], cb_tmp[:, 0:1], cb_tmp[:, 1:2], ALU.max))
            alone(dve.reciprocal(cb_tmp[:, 3:4], cb_tmp[:, 2:3]))
            alone(dve.tensor_scalar(cb[:, :], cb[:, :], cb_tmp[:, 3:4], None, ALU.mult))
            alone(dve.tensor_tensor(rises[:, :], cb[:, 1:LEVELS], cb[:, 0:CUTS], ALU.subtract))
            alone(dve.tensor_tensor(cuts[:, :], cb[:, 1:LEVELS], cb[:, 0:CUTS], ALU.add))
            alone(dve.tensor_scalar(cuts[:, :], cuts[:, :], 0.5, None, ALU.mult))
            def keep(j, op, k):
                alone(dve.tensor_tensor(cuts[:, j:j + 1], cuts[:, j:j + 1], cuts[:, k:k + 1], op))

            keep(1, ALU.min, 3)
            keep(5, ALU.max, 3)
            keep(0, ALU.min, 1)
            keep(2, ALU.max, 1)
            keep(2, ALU.min, 3)
            keep(4, ALU.max, 3)
            keep(4, ALU.min, 5)
            keep(6, ALU.max, 5)
            dve.wait_ge(scale_ready, 1)
            alone(dve.reciprocal(inv_scale[:, :], scale[:, :]))
            dve.wait_ge(loaded["ffn_scal"], 32)
            dve.tensor_scalar(ffn_scal[:, 2:3], ffn_scal[:, 0:1], EXPERT_SCALE, None, ALU.mult).then_inc(scal_ready, 1)

            dve.wait_ge(lora_bT_hi_ready, 2)
            dve.tensor_tensor(lora_bT[RANK:P, :], psum[0][RANK:P, :], lora_bT_tmp[RANK:P, :], ALU.subtract)\
               .then_inc(lora_bT_ready, 1)

            dve.wait_ge(loaded["qweight"], 16)
            dve.tensor_scalar(q_nat[:, :, :], q_nat[:, :, :].bitcast(I32), ffn_scal[:, 1:2], None, ALU.subtract)\
               .then_inc(qmz_ready, 1)
            dve.wait_ge(xT_ready, CT)
            dve.tensor_copy(xT_hi[:, :, 0:HT], xT[:, :, 0:HT]).then_inc(xT_hi_ready, 1)
            for o in range(CT):
                dve.wait_ge(dT_hi_ready, o + 1)
                dve.tensor_tensor(split_b_lo[:, o, :], psum[1 + o][:, :], split_b_hi[:, o, :], ALU.subtract)\
                   .then_inc(dT_lo_ready, 1)

            def blocks(ap):
                return ap.rearrange("p (b n) -> p b n", n=P)

            GB = 2 * CT

            def per_block(ap, h):
                return ap[:, GB * h:GB * (h + 1)].unsqueeze(2).to_broadcast([P, GB, P])

            for h in range(HALVES):
                dve.wait_ge(loaded[f"cond_w{h}"], 16)
                dve.wait_ge(delta_ready, 2 * (h + 1))
                last = mark(dve.tensor_tensor(cond_n[:, h, :], cond_n[:, h, :], delta[:, h, :], ALU.add))
            for h in range(HALVES):
                dve.wait_ge(dve_step, last - 1 + h)
                norm = mark(dve.tensor_tensor(blocks(cond_n[:, h, :]), blocks(cond_n[:, h, :]),
                                              per_block(inv_scale, h), ALU.mult))

            done_add = {}

            def cut_step(j):
                made = {}
                for h in range(HALVES):
                    if j == 0:
                        dve.wait_ge(dve_step, norm - 1 + h)
                    elif j >= 2:
                        dve.wait_ge(dve_step, done_add[h])
                    dst = acc if j == 0 else step
                    made[h] = mark(dve.tensor_scalar(dst[:, h, :], cond_n[:, h, :], cuts[:, j:j + 1],
                                                     rises[:, j:j + 1], ALU.is_gt, ALU.mult))
                if j:
                    for h in range(HALVES):
                        dve.wait_ge(dve_step, made[h])
                        done_add[h] = mark(dve.tensor_tensor(acc[:, h, :], acc[:, h, :], step[:, h, :], ALU.add))

            cut_step(0)
            cut_step(1)

            dve.wait_ge(woT_ready, 1)
            dve.tensor_copy(woT_hi[:, :, :], woT[:, :, :]).then_inc(woT_hi_ready, 1)
            dve.wait_ge(hlT_ready, 3)
            one = mark(dve.tensor_copy(boR[:, :, :], bo_col.unsqueeze(2).to_broadcast([P, CT, P])))
            dve.wait_ge(woT_hi_ready, 1)
            dve.tensor_tensor(woT_lo[:, :, :], woT[:, :, :], woT_hi[:, :, :], ALU.subtract).then_inc(woT_lo_ready, 1)
            dve.wait_ge(dve_step, one)
            one = mark(dve.tensor_copy(boR_hi[:, :, :], boR[:, :, :]))
            cut_step(2)
            dve.wait_ge(dve_step, one)
            dve.tensor_tensor(boR_lo[:, :, :], boR[:, :, :], boR_hi[:, :, :], ALU.subtract).then_inc(boR_ready, 1)
            cut_step(3)
            dve.wait_ge(xT_ready, 2 * CT)
            dve.tensor_copy(xT_hi[:, :, HT:2 * HT], xT[:, :, HT:2 * HT]).then_inc(xT_hi_ready, 1)
            cut_step(4)
            dve.wait_ge(Bf_ready, 1)
            one = mark(dve.tensor_copy(Bf_hi[:, :], Bf[:, :]))
            cut_step(5)
            dve.wait_ge(dve_step, one)
            dve.tensor_tensor(Bf_lo[:, :], Bf[:, :], Bf_hi[:, :], ALU.subtract).then_inc(Bf_lo_ready, 1)
            dve.wait_ge(woG_hi_ready, 1)
            dve.tensor_tensor(woG_lo[:, :], psum[5][:, :], woG_hi[:, :], ALU.subtract).then_inc(woG_lo_ready, 1)
            dve.wait_ge(boG_done, 1)
            dve.wait_ge(loaded["ffn_bias"], 16)
            dve.tensor_tensor(y_bias[:, :], psum[7][:, :], ffn_bias_bc[:, :], ALU.add).then_inc(y_bias_ready, 1)

            dve.wait_ge(loaded["lang"], 16)
            alone(dve.tensor_copy(lang_f[:, :], lang_i[:, :]))
            dve.wait_ge(ident_ready, 1 + E)
            alone(dve.tensor_tensor(lang_hot[:, :, :], lang_f[:, :].unsqueeze(2).to_broadcast([P, BATCH, E]),
                                    expert_no[:, :].unsqueeze(1).to_broadcast([P, BATCH, E]), ALU.is_equal))
            alone(dve.tensor_scalar(lang_hot[:, :, :], lang_hot[:, :, :], LANG_BIAS, None, ALU.mult))

            def hl_x(pair, bank):
                dve.wait_ge(xhl_done, pair + 1)
                dve.wait_ge(woHL_ready, 2)
                t = 2 * pair
                one = mark(dve.tensor_tensor(hl[:, t:t + 2, :], psum[bank][:, 0:2 * HL].rearrange("p (t n) -> p t n", t=2),
                                             hl_bias[:, :].unsqueeze(1).to_broadcast([P, 2, HL]), ALU.add))
                dve.wait_ge(dve_step, one)
                dve.tensor_tensor(hl[:, t:t + 2, ER:HL], hl[:, t:t + 2, ER:HL], lang_hot[:, t:t + 2, :], ALU.add)\
                   .then_inc(hl_x_ready, 1)

            hl_x(0, 0)
            hl_x(1, 1)
            cut_step(6)

            for h in range(HALVES):
                dve.wait_ge(dve_step, done_add[h])
                one = mark(dve.scalar_tensor_tensor(blocks(step[:, h, :]), blocks(acc[:, h, :]), cb[:, 0:1],
                                                    per_block(scale, h), ALU.add, ALU.mult))
                dve.wait_ge(dve_step, one)
                dve.tensor_tensor(acc[:, h, :], step[:, h, :], delta[:, h, :], ALU.add).then_inc(w_eff_ready, 1)
            for i in range(CT):
                dve.wait_ge(M_hi_ready, i + 1)
                dve.tensor_tensor(split_b_lo[:, i, 0:3 * D], psum[i][:, 0:3 * D], split_b_hi[:, i, 0:3 * D],
                                  ALU.subtract).then_inc(M_lo_ready, 1)

            def softmax_max(h, bank):
                dve.wait_ge(scores_done, h + 1)
                m = neg_max[:, TPH * h:TPH * (h + 1)]
                alone(dve.tensor_reduce(m, psum[bank][:, :].rearrange("p (b k) -> p b k", b=TPH), AX.X, ALU.max))
                dve.tensor_scalar(m, m, -SOFTMAX_SCALE, None, ALU.mult).then_inc(max_ready, 1)

            def softmax_norm(h):
                dve.wait_ge(exp_ready, TPH * (h + 1))
                s = row_sum[:, TPH * h:TPH * (h + 1)]
                alone(dve.reciprocal(s, s))
                pr = probs[:, h, :].rearrange("p (b k) -> p b k", b=TPH)
                dve.tensor_tensor(pr, pr, s.unsqueeze(2).to_broadcast([P, TPH, P]), ALU.mult).then_inc(probs_ready, 1)

            def o_lo(h):
                dve.wait_ge(oT_hi_ready, h + 1)
                dve.tensor_tensor(oT_lo[:, h, :], oT[:, h, :], oT_hi[:, h, :], ALU.subtract).then_inc(oT_lo_ready, 1)

            def gating(h, banks):
                t0 = TPH * h
                T = slice(t0, t0 + TPH)
                for pair in range(2):
                    dve.wait_ge(hl_done, 2 * h + pair + 1)
                    dve.wait_ge(hl_x_ready, 2 * h + pair + 1)
                    p = hl[:, t0 + 2 * pair:t0 + 2 * pair + 2, :]
                    dve.tensor_tensor(p, psum[banks[pair]][:, 0:2 * HL].rearrange("p (t n) -> p t n", t=2), p, ALU.add)\
                       .then_inc(hl_read, 1)
                for t in range(t0, t0 + TPH):
                    dve.wait_ge(hl_read, 2 * h + (t - t0) // 2 + 1)
                    last = mark(dve.max(top[:, t, :], hl[:, t, ER:HL]))
                dve.wait_ge(dve_step, last)
                dve.tensor_tensor(top_exp[:, T], top[:, T, 1], top[:, T, 0], ALU.subtract).then_inc(top_diff_ready, 1)
                for t in range(t0, t0 + TPH):
                    last = mark(dve.max_index(top_at[:, t, :], top[:, t, :], hl[:, t, ER:HL]))
                dve.wait_ge(dve_step, last)
                nos = expert_no[:, :].unsqueeze(1).to_broadcast([P, TPH, E])

                def over_experts(ap):
                    return ap.unsqueeze(2).to_broadcast([P, TPH, E])

                mark(dve.tensor_tensor(gate[:, T, :], nos, over_experts(top_at[:, T, 0]), ALU.is_equal))
                hot = mark(dve.tensor_tensor(gate2[:, T, :], nos, over_experts(top_at[:, T, 1]), ALU.is_equal))
                dve.wait_ge(top_exp_ready, h + 1)
                alone(dve.tensor_scalar(w_first[:, T], top_exp[:, T], 1.0, None, ALU.add))
                alone(dve.reciprocal(w_first[:, T], w_first[:, T]))
                one = mark(dve.tensor_tensor(w_second[:, T], w_first[:, T], top_exp[:, T], ALU.mult))
                dve.wait_ge(dve_step, hot)
                mark(dve.tensor_tensor(gate[:, T, :], gate[:, T, :], over_experts(w_first[:, T]), ALU.mult))
                dve.wait_ge(dve_step, one)
                alone(dve.tensor_tensor(gate2[:, T, :], gate2[:, T, :], over_experts(w_second[:, T]), ALU.mult))
                alone(dve.tensor_tensor(gate[:, T, :], gate[:, T, :], gate2[:, T, :], ALU.add))
                dve.tensor_tensor(gh[:, h, :].rearrange("p (t e r) -> p t e r", t=TPH, e=E),
                                  hl[:, T, 0:ER].rearrange("p t (e r) -> p t e r", e=E),
                                  gate[:, T, :].unsqueeze(3).to_broadcast([P, TPH, E, R]), ALU.mult)\
                   .then_inc(gh_ready, 1)

            def gh_lo(h, bank):
                dve.wait_ge(ghT_hi_ready, h + 1)
                dve.tensor_tensor(ghT_lo[:, h, :], psum[bank][:, :], ghT_hi[:, h, :], ALU.subtract)\
                   .then_inc(ghT_lo_ready, 1)

            def y_store(t):
                dve.wait_ge(y_done, t + 1)
                dve.wait_ge(y_bias_ready, 1)
                dve.tensor_tensor(y_out[:, t, :], psum[4 + t % 4][:, :], y_bias[:, :], ALU.add).then_inc(y_ready, 1)

            softmax_max(0, 0)
            softmax_norm(0)
            o_lo(0)
            gating(0, (3, 0))
            softmax_max(1, 1)
            hl_x(2, 2)
            hl_x(3, 3)
            gh_lo(0, 0)
            softmax_norm(1)
            for t in range(TPH):
                y_store(t)
            o_lo(1)
            gating(1, (3, 0))
            gh_lo(1, 1)
            for t in range(TPH, BATCH):
                y_store(t)

        @block.tensor
        def _(pe):
            def three(out_ap, l_hi, l_lo, r_hi, r_lo, first, last):
                pe.matmul(out_ap, l_hi, r_hi, start=first, stop=False)
                pe.matmul(out_ap, l_hi, r_lo, start=False, stop=False)
                return pe.matmul(out_ap, l_lo, r_hi, start=False, stop=last)

            pe.wait_ge(ident_ready, 1)
            pe.wait_ge(loaded["lora_b"], 32)
            for o in range(CT):
                mm = pe.transpose(psum[0][:, o * P:(o + 1) * P],
                                  lora_b_dup[:, o, :, :].rearrange("p a r -> p (a r)"), ident[:, :])
            mm.then_inc(lora_bT_done, 1)

            def x_transposes(h, banks):
                for c in range(CT):
                    for t in range(TPH):
                        mm = pe.transpose(psum[banks[c]][:, t * P:(t + 1) * P],
                                          x_nat[:, TPH * h + t, c * P:(c + 1) * P], ident[:, :])
                    mm.then_inc(xT_done, 1)

            pe.wait_ge(loaded["x0"], 16)
            x_transposes(0, (1, 2, 3, 4))

            pe.wait_ge(lora_bT_hi_ready, 2)
            pe.wait_ge(lora_bT_ready, 1)
            pe.wait_ge(lora_a_lo_ready, 1)
            for o, b in enumerate((5, 6, 7, 0)):
                pe.matmul(psum[b][:, :], lora_bT[:, o * P:(o + 1) * P], lora_a_hi[:, :], start=True, stop=False)
                pe.matmul(psum[b][:, :], lora_bT[:, o * P:(o + 1) * P], lora_a_lo[:, :], start=False, stop=True)\
                  .then_inc(delta_done, 1)

            pe.wait_ge(qmz_ready, 1)
            for o in range(CT):
                pe.wait_ge(xT_ready, o + 1)
                for n in range(CT):
                    mm = pe.transpose(psum[1 + o][:, n * P:(n + 1) * P], q_nat[:, n, o * P:(o + 1) * P], ident[:, :])
                mm.then_inc(dT_done, 1)

            pe.wait_ge(loaded["exp_a"], 16)
            pe.wait_ge(loaded["router"], 16)
            pe.wait_ge(loaded["wo"], 16)
            pe.wait_ge(delta_ready, 1)
            for c in range(CT):
                mm = pe.transpose(psum[5][:, c * P:(c + 1) * P], expa_nat[:, c * P:(c + 1) * P], ident[:, :])
            mm.then_inc(hlT_done, 1)
            pe.wait_ge(delta_ready, 2)
            for c in range(CT):
                mm = pe.transpose(psum[6][:, c * E:(c + 1) * E], router_nat[:, c * P:(c + 1) * P], ident[0:E, 0:E])
            pe.wait_ge(loaded["biases"], 32)
            mm = pe.transpose(psum[6][:, CT * E:CT * E + 3 + CT], bias_rows[:, :], ident[0:3 + CT, 0:3 + CT])
            mm.then_inc(hlT_done, 1)
            pe.wait_ge(delta_ready, 3)
            for c in range(CT):
                mm = pe.transpose(psum[7][:, c * P:(c + 1) * P], wo_nat[:, c * P:(c + 1) * P], ident[:, :])
            mm.then_inc(woT_done, 1)

            pe.wait_ge(delta_ready, 4)
            pe.wait_ge(hlT_ready, 3)
            pe.wait_ge(woT_ready, 1)
            pe.wait_ge(loaded["x1"], 16)
            x_transposes(1, (0, 5, 6, 7))

            for o in range(CT):
                pe.wait_ge(moe_split_ready, o + 1)
                pe.wait_ge(dT_lo_ready, o + 1)
                if o == 0:
                    pe.wait_ge(dT_lo_ready, CT)
                for i in range(CT):
                    s = slice(i * P, (i + 1) * P)
                    mm = three(psum[1 + i][:, :], split_a_hi[:, o, s], split_a_lo[:, o, s],
                               split_b_hi[:, o, :], split_b_lo[:, o, :], o == 0, o == CT - 1)
                    if o == CT - 1:
                        mm.then_inc(G_done, 1)
            pe.wait_ge(expb_ready, 1)
            pe.wait_ge(xT_ready, CT + 1)
            for o in range(CT):
                mm = three(psum[0][:, :], expb_hi[:, o, :], expb_lo[:, o, :], split_b_hi[:, o, :],
                           split_b_lo[:, o, :], o == 0, o == CT - 1)
            mm.then_inc(Bf_done, 1)
            pe.wait_ge(xT_ready, 2 * CT)
            for c in range(CT):
                mm = pe.matmul(psum[6][:, 0:HL], woT[:, c, :], hlT[:, c, :], start=(c == 0), stop=(c == CT - 1))
            mm.then_inc(woHL_done, 1)
            pe.wait_ge(woHL_ready, 1)
            pe.wait_ge(boR_ready, 1)
            for c in range(CT):
                mm = pe.matmul(psum[6][:, 256:256 + HL], boR[:, c, :], hlT[:, c, :], start=(c == 0), stop=(c == CT - 1))
            mm.then_inc(woHL_done, 1)

            def x_hl(pair, bank):
                for t in range(2):
                    for c in range(CT):
                        s = slice((2 * pair + t) * SEQ, (2 * pair + t + 1) * SEQ)
                        mm = pe.matmul(psum[bank][:, t * HL:(t + 1) * HL], xT[:, c, s], hlT[:, c, :],
                                       start=(c == 0), stop=(c == CT - 1))
                mm.then_inc(xhl_done, 1)

            pe.wait_ge(woT_lo_ready, 1)
            for c in range(CT):
                pe.wait_ge(G_hi_ready, c + 1)
                pe.wait_ge(G_lo_ready, c + 1)
                mm = three(psum[5][:, :], woT_hi[:, c, :], woT_lo[:, c, :], G_hi[:, c, :], G_lo[:, c, :],
                           c == 0, c == CT - 1)
            mm.then_inc(woG_done, 1)
            for c in range(CT):
                mm = three(psum[7][:, :], boR_hi[:, c, :], boR_lo[:, c, :], G_hi[:, c, :], G_lo[:, c, :],
                           c == 0, c == CT - 1)
            mm.then_inc(boG_done, 1)
            pe.wait_ge(Bf_ready, 1)
            x_hl(0, 0)
            x_hl(1, 1)

            def y_x(t):
                for c in range(CT):
                    s = slice(t * SEQ, (t + 1) * SEQ)
                    three(psum[4 + t % 4][:, :], xT_hi[:, c, s], xT_lo[:, c, s], G_hi[:, c, :], G_lo[:, c, :],
                          c == 0, False)

            def y_o(t):
                h, s = t // TPH, slice((t % TPH) * SEQ, (t % TPH + 1) * SEQ)
                three(psum[4 + t % 4][:, :], oT_hi[:, h, s], oT_lo[:, h, s], woG_hi[:, :], woG_lo[:, :], False, False)

            def y_gh(t):
                h, s = t // TPH, slice((t % TPH) * SEQ, (t % TPH + 1) * SEQ)
                three(psum[4 + t % 4][:, :], ghT_hi[:, h, s], ghT_lo[:, h, s], Bf_hi[:, :], Bf_lo[:, :], False, True)\
                    .then_inc(y_done, 1)

            pe.wait_ge(xT_hi_ready, 1)
            pe.wait_ge(xT_lo_ready, CT)
            y_x(0)
            pe.wait_ge(woG_lo_ready, 1)
            y_x(1)
            pe.wait_ge(woHL_ready, 2)
            y_x(2)
            pe.wait_ge(y_bias_ready, 1)
            y_x(3)

            pe.wait_ge(hl_x_ready, 2)
            for o in range(CT):
                pe.wait_ge(wqkv_ready, o + 1)
                pe.wait_ge(w_eff_hi_ready, o // 2 + 1)
                pe.wait_ge(w_eff_lo_ready, o // 2 + 1)
                for i in range(CT):
                    s = slice(i * P, (i + 1) * P)
                    mm = three(psum[i][:, 0:3 * D], split_a_hi[:, o, s], split_a_lo[:, o, s], wqkv_hi[:, o, :],
                               wqkv_lo[:, o, :], o == 0, o == CT - 1)
                    if o == CT - 1:
                        mm.then_inc(M_done, 1)

            def qkv(h, which, bank):
                for i in range(CT):
                    m = slice(which * D, (which + 1) * D)
                    s = slice(h * HT, (h + 1) * HT)
                    mm = three(psum[bank][:, :], split_b_hi[:, i, m], split_b_lo[:, i, m], xT_hi[:, i, s],
                               xT_lo[:, i, s], i == 0, i == CT - 1)
                mm.then_inc(qkvT_done, 1)

            def v_rows(h, bank):
                for b in range(TPH):
                    mm = pe.transpose(psum[bank][:, b * P:(b + 1) * P], vT[:, h, b * P:(b + 1) * P], ident[:, :])
                mm.then_inc(v_done, 1)

            def scores(h, bank):
                for b in range(TPH):
                    s = slice(b * P, (b + 1) * P)
                    mm = pe.matmul(psum[bank][:, s], qT[:, h, s], kT[:, h, s], start=True, stop=True)
                mm.then_inc(scores_done, 1)

            def probs_turn(h, bank):
                pe.wait_ge(probs_ready, h + 1)
                for b in range(TPH):
                    s = slice(b * P, (b + 1) * P)
                    mm = pe.transpose(psum[bank][:, s], probs[:, h, s], ident[:, :])
                mm.then_inc(probsT_done, 1)

            def attend(h, bank):
                pe.wait_ge(probsT_ready, h + 1)
                pe.wait_ge(v_ready, h + 1)
                for b in range(TPH):
                    s = slice(b * P, (b + 1) * P)
                    mm = pe.matmul(psum[bank][:, s], v[:, h, s], probsT[:, h, s], start=True, stop=True)
                mm.then_inc(oT_done, 1)

            def o_hl(h, pair, bank):
                for t in range(2):
                    s = slice((2 * pair + t) * P, (2 * pair + t + 1) * P)
                    mm = pe.matmul(psum[bank][:, t * HL:(t + 1) * HL], oT[:, h, s], woHL[:, :], start=True, stop=True)
                mm.then_inc(hl_done, 1)

            def gh_turn(h, bank):
                pe.wait_ge(gh_ready, h + 1)
                for b in range(TPH):
                    s = slice(b * P, (b + 1) * P)
                    mm = pe.transpose(psum[bank][:, s], gh[:, h, s], ident[:, :])
                mm.then_inc(ghT_done, 1)

            pe.wait_ge(M_hi_ready, CT)
            pe.wait_ge(M_lo_ready, CT)
            qkv(0, 2, 0)
            qkv(0, 0, 1)
            qkv(0, 1, 2)
            pe.wait_ge(qkvT_ready, 1)
            v_rows(0, 3)
            pe.wait_ge(qkvT_ready, 3)
            scores(0, 0)
            pe.wait_ge(xT_hi_ready, 2)
            pe.wait_ge(xT_lo_ready, 2 * CT)
            qkv(1, 2, 1)
            pe.wait_ge(qkvT_ready, 4)
            v_rows(1, 2)
            pe.wait_ge(v_ready, 1)
            probs_turn(0, 3)
            pe.wait_ge(exp_ready, TPH)
            qkv(1, 0, 0)
            attend(0, 1)
            pe.wait_ge(v_ready, 2)
            qkv(1, 1, 2)
            pe.wait_ge(oT_ready, 1)
            pe.wait_ge(woHL_ready, 1)
            pe.wait_ge(probsT_ready, 1)
            o_hl(0, 0, 3)
            pe.wait_ge(qkvT_ready, 5)
            o_hl(0, 1, 0)
            pe.wait_ge(oT_hi_ready, 1)
            pe.wait_ge(oT_lo_ready, 1)
            for t in range(TPH):
                y_o(t)
            pe.wait_ge(qkvT_ready, 6)
            scores(1, 1)
            x_hl(2, 2)
            pe.wait_ge(hl_read, 1)
            x_hl(3, 3)
            pe.wait_ge(hl_read, 2)
            gh_turn(0, 0)
            pe.wait_ge(ghT_hi_ready, 1)
            pe.wait_ge(ghT_lo_ready, 1)
            pe.wait_ge(Bf_lo_ready, 1)
            for t in range(TPH):
                y_gh(t)
            pe.wait_ge(exp_ready, 2 * TPH)
            probs_turn(1, 1)
            pe.wait_ge(y_ready, 1)
            y_x(4)
            pe.wait_ge(hl_x_ready, 3)
            attend(1, 2)
            pe.wait_ge(y_ready, 2)
            y_x(5)
            pe.wait_ge(oT_ready, 2)
            pe.wait_ge(hl_x_ready, 4)
            o_hl(1, 0, 3)
            o_hl(1, 1, 0)
            pe.wait_ge(oT_hi_ready, 2)
            pe.wait_ge(oT_lo_ready, 2)
            y_o(4)
            y_o(5)
            pe.wait_ge(y_ready, 3)
            y_x(6)
            y_o(6)
            pe.wait_ge(y_ready, 4)
            y_x(7)
            y_o(7)
            pe.wait_ge(probsT_ready, 2)
            gh_turn(1, 1)
            pe.wait_ge(ghT_hi_ready, 2)
            pe.wait_ge(ghT_lo_ready, 2)
            for t in range(TPH, BATCH):
                y_gh(t)


_INPUTS = ["x", "condB_codebook", "itok_B_0_7", "L0_cond_weight", "L0_cond_scale_log", "L0_cond_lora_A",
           "L0_cond_lora_B", "L0_attn_Wqkv", "L0_attn_bqkv", "L0_attn_Wo", "L0_attn_bo", "L0_cond2_W",
           "L0_cond2_Wr", "L0_cond2_A", "L0_cond2_B", "L0_ffn_qweight", "L0_ffn_scale",
           "L0_ffn_zero_point", "L0_ffn_bias"]
_SHAPES = {"L0_cond_scale_log": (512, 4), "L0_ffn_scale": (1,), "L0_ffn_zero_point": (1,)}


def kernel(**inputs):
    import numpy as np
    import concourse.bacc as bacc
    from concourse.bass_utils import run_bass_kernel_spmd

    nc = bacc.Bacc("TRN2", target_bir_lowering=False, num_devices=1)
    arrays, args = {}, []
    for name in _INPUTS:
        a = np.ascontiguousarray(inputs[name])
        a = a.reshape(_SHAPES.get(name, a.shape))
        arrays[f"in_{name}"] = a
        args.append(nc.dram_tensor(f"in_{name}", a.shape, mybir.dt.from_np(a.dtype), kind="ExternalInput").ap())
    out = nc.dram_tensor("out", arrays["in_x"].shape, F32, kind="ExternalOutput").ap()
    block_kernel(nc, *args, out)
    result = run_bass_kernel_spmd(nc, [arrays], core_ids=[0])
    return result.results[0]["out"]
```

```python
from contextlib import ExitStack

import concourse.bass as bass
from concourse import mybir

F32 = mybir.dt.float32
F32R = mybir.dt.float32r
I32 = mybir.dt.int32
U32 = mybir.dt.uint32
ALU = mybir.AluOpType
ACT = mybir.ActivationFunctionType
AX = mybir.AxisListType

P = 128


def block_kernel(nc, small_in, lora_in, hl_t, x_t, cond_w, q_t, moe_w, wo_t, exp_b, wqkv, ffn_bias, lang, out):
    BATCH, SEQ, C = out.shape
    CT = C // P
    HALVES = 2
    TPH = BATCH // HALVES
    HT = TPH * SEQ
    PAIRS = BATCH // 2
    PT = 2 * SEQ
    D = wo_t.shape[2]
    RANK = P // 2
    E, R = 8, 16
    ER = E * R
    HL = hl_t.shape[2]
    LEVELS = 8
    CUTS = LEVELS - 1
    GROUPS = CT * CT
    SOFTMAX_SCALE = float(D) ** -0.5
    LORA_SCALE = 32.0 / 64.0
    LANG_BIAS = 5.0
    EXPERT_SCALE = 32.0 / 16.0
    CODEBOOK_FLOOR = 1e-8
    WARM_UP = 20
    X_LOADS = ("x_first", "x_second", "x1", "x1", "x2", "x2", "x2", "x2")
    HL_PARTS = ((0, 1), (2, 3), (4,), (5, 6, 7))
    assert SEQ == P and D == P and ER == P and HL == ER + E and HT == 512 and C == 512
    assert x_t.shape == (PAIRS, P, CT, PT)

    with ExitStack() as ctx:
        def sb(name, shape, dt=F32):
            return ctx.enter_context(nc.sbuf_tensor(name, shape, dt))

        def sem(name):
            return ctx.enter_context(nc.semaphore(name))

        SMALL = small_in.shape[1]
        small = sb("small", [P, SMALL])
        cb, ffn_scal = small[:, 0:LEVELS], small[:, LEVELS:LEVELS + 1]
        zero_point = small[:, LEVELS + 1:LEVELS + 2]
        qkv_bias, bo_col = small[:, LEVELS + 2:LEVELS + 5], small[:, LEVELS + 5:LEVELS + 5 + CT]
        scale = small[:, SMALL - GROUPS:SMALL]
        inv_scale = sb("inv_scale", [P, GROUPS])
        low_scaled = sb("low_scaled", [P, GROUPS])
        ffn_scal2 = sb("ffn_scal2", [P, 1])
        minus_zero = sb("minus_zero", [P, 1])
        ffn_bias_bc = sb("ffn_bias_bc", [P, C])
        lang_i = sb("lang_i", [P, BATCH], I32)
        cb_tmp = sb("cb_tmp", [P, 4])
        levels = sb("levels", [P, LEVELS])
        cuts = sb("cuts", [P, CUTS])
        minus_cut = sb("minus_cut", [P, 1])
        rises = sb("rises", [P, CUTS])
        ident = sb("ident", [P, P])
        lora = sb("lora", [P, 2, C])
        lora_bT = sb("lora_bT", [P, C], F32R)
        lora_a_hi = sb("lora_a_hi", [P, C], F32R)
        lora_a_lo = sb("lora_a_lo", [P, C], F32R)
        hlT = sb("hlT", [P, CT, HL])
        xT = sb("xT", [P, PAIRS, CT, PT])
        xT_hi = sb("xT_hi", [P, CT, BATCH * SEQ], F32R)
        xT_lo = sb("xT_lo", [P, CT, BATCH * SEQ], F32R)
        cond_n = sb("cond_n", [P, CT, C])
        q_i = sb("q_i", [P, CT, C], I32)
        moe = sb("moe", [P, CT, C])
        wqkv_n = sb("wqkv_n", [P, CT, 3 * D])
        split_a_hi = sb("split_a_hi", [P, CT, C], F32R)
        split_a_lo = sb("split_a_lo", [P, CT, C], F32R)
        split_b_hi = sb("split_b_hi", [P, CT, C], F32R)
        split_b_lo = sb("split_b_lo", [P, CT, C], F32R)
        G_hi = sb("G_hi", [P, CT, C], F32R)
        G_lo = sb("G_lo", [P, CT, C], F32R)
        wqkv_hi = sb("wqkv_hi", [P, CT, 3 * D], F32R)
        wqkv_lo = sb("wqkv_lo", [P, CT, 3 * D], F32R)
        expb = sb("expb", [P, CT, ER])
        expb_hi = sb("expb_hi", [P, CT, ER], F32R)
        expb_lo = sb("expb_lo", [P, CT, ER], F32R)
        woT = sb("woT", [P, CT, D])

        def as_tiles(ap):
            return ap.rearrange("p (t n) -> p t n", t=CT)

        def as_row(ap):
            return ap.rearrange("p t n -> p (t n)")

        woT_hi = as_tiles(sb("woT_hi", [P, C], F32R)[:, :])
        woT_lo = as_tiles(lora_bT[:, :])
        ones = sb("ones", [P, P])
        ones_r = sb("ones_r", [P, P], F32R)
        bo_G = sb("bo_G", [P, C])
        bo_G_hi = lora_a_hi
        bo_G_lo = lora_a_lo
        bo_HL = sb("bo_HL", [P, HL])
        Bf = as_row(expb[:, :, :])
        Bf_hi = sb("Bf_hi", [P, C], F32R)
        Bf_lo = sb("Bf_lo", [P, C], F32R)
        woG = lora[:, 0, :]
        woG_hi = as_row(expb_hi[:, :, :])
        woG_lo = as_row(expb_lo[:, :, :])
        woHL = sb("woHL", [D, HL])
        boG = lora[:, 1, :]
        y_bias = ffn_bias_bc
        hl_bias = sb("hl_bias", [P, HL])
        delta = sb("delta", [P, CT, C])
        cond_work = sb("cond_work", [P, 2, CT, C])
        acc = cond_work[:, 0, :, :]
        step = cond_work[:, 1, :, :]
        above = q_i[:, 2:4, :].bitcast(F32)

        def place(ap, n):
            return ap[:, 2 * n:2 * n + 2, :]

        qT, kT = place(cond_n, 0), place(cond_n, 1)
        vT, v = place(delta, 0), place(delta, 1)
        probs, probsT = place(moe, 0), place(moe, 1)
        oT, gh = place(q_i, 0).bitcast(F32), place(q_i, 1).bitcast(F32)
        oT_hi, ghT_hi = place(split_a_hi, 0), place(split_a_hi, 1)
        oT_lo, ghT_lo = place(split_a_lo, 0), place(split_a_lo, 1)
        neg_max = sb("neg_max", [P, BATCH])
        row_sum = sb("row_sum", [P, BATCH])
        hl = sb("hl", [P, BATCH, HL])
        lang_f = sb("lang_f", [P, BATCH])
        lang_hot = sb("lang_hot", [P, BATCH, E])
        expert_no = sb("expert_no", [P, E])
        top = sb("top", [P, BATCH, 8])
        top_at = sb("top_at", [P, BATCH, 8], U32)
        top_exp = sb("top_exp", [P, BATCH])
        weight = sb("weight", [P, BATCH])
        gate = sb("gate", [P, BATCH, E])
        gate2 = sb("gate2", [P, BATCH, E])
        y_out = cond_work[:, :, :, :].rearrange("p a t c -> p (a t) c")

        psum = [ctx.enter_context(nc.psum_tensor(f"psum{b}", [P, 512], F32)) for b in range(8)]

        LOADS = (["small", "lora_b", "lora_a", "hlT", "x_first", "x_second", "x1", "x2", "woT", "exp_b", "wqkv", "ffn_bias", "lang"]
                 + [f"{n}{o}" for n in ("q", "moe") for o in range(CT)] + ["cond_w0", "cond_w1"])
        loaded = {n: sem(f"ld_{n}") for n in LOADS}
        delta_done = sem("delta_done")
        G_done = sem("G_done")
        Bf_done = sem("Bf_done")
        woG_done = sem("woG_done")
        woHL_done = sem("woHL_done")
        boG_done = sem("boG_done")
        boHL_done = sem("boHL_done")
        xhl_done = sem("xhl_done")
        M_done = sem("M_done")
        qkvT_done = sem("qkvT_done")
        v_done = sem("v_done")
        scores_done = sem("scores_done")
        probsT_done = sem("probsT_done")
        oT_done = sem("oT_done")
        hl_done = sem("hl_done")
        ghT_done = sem("ghT_done")
        y_done = sem("y_done")
        scale_ready = sem("scale_ready")
        lora_b_hi_ready = sem("lora_b_hi_ready")
        delta_ready = sem("delta_ready")
        moe_hi_ready = sem("moe_hi_ready")
        qmz_hi_ready = sem("qmz_hi_ready")
        norm_ready = sem("norm_ready")
        expb_hi_ready = sem("expb_hi_ready")
        woT_hi_ready = sem("woT_hi_ready")
        xT_hi_ready = sem("xT_hi_ready")
        G_ready = sem("G_ready")
        G_hi_ready = sem("G_hi_ready")
        hl_raw_ready = sem("hl_raw_ready")
        Bf_ready = sem("Bf_ready")
        woG_ready = sem("woG_ready")
        woHL_ready = sem("woHL_ready")
        boG_ready = sem("boG_ready")
        hl_bias_ready = sem("hl_bias_ready")
        delta_low_ready = sem("delta_low_ready")
        wqkv_hi_ready = sem("wqkv_hi_ready")
        above_ready = sem("above_ready")
        w_eff_hi_ready = sem("w_eff_hi_ready")
        M_hi_ready = sem("M_hi_ready")
        qkvT_ready = sem("qkvT_ready")
        v_ready = sem("v_ready")
        exp_ready = sem("exp_ready")
        probsT_ready = sem("probsT_ready")
        oT_ready = sem("oT_ready")
        oT_hi_ready = sem("oT_hi_ready")
        top_exp_ready = sem("top_exp_ready")
        ghT_hi_ready = sem("ghT_hi_ready")
        dve_step = sem("dve_step")
        levels_ready = sem("levels_ready")
        rises_ready = sem("rises_ready")
        lang_hot_ready = sem("lang_hot_ready")
        inv_scale_ready = sem("inv_scale_ready")
        ffn_scal2_ready = sem("ffn_scal2_ready")
        lora_a_hi_ready = sem("lora_a_hi_ready")
        lora_lo_ready = sem("lora_lo_ready")
        minus_zero_ready = sem("minus_zero_ready")
        qmz_ready = sem("qmz_ready")
        wd_ready = sem("wd_ready")
        norm_half_ready = sem("norm_half_ready")
        step_ready = sem("step_ready")
        w_eff_ready = sem("w_eff_ready")
        w_eff_lo_ready = sem("w_eff_lo_ready")
        minus_cut_ready = sem("minus_cut_ready")
        bo_G_ready = sem("bo_G_ready")
        bo_HL_ready = sem("bo_HL_ready")
        M_lo_ready = sem("M_lo_ready")
        max_ready = sem("max_ready")
        probs_ready = sem("probs_ready")
        oT_lo_ready = sem("oT_lo_ready")
        logits_ready = sem("logits_ready")
        hl_read = sem("hl_read")
        top_diff_ready = sem("top_diff_ready")
        gh_ready = sem("gh_ready")
        ghT_lo_ready = sem("ghT_lo_ready")
        y_ready = sem("y_ready")
        pool_step = sem("pool_step")
        ident_ready = sem("ident_ready")
        ones_ready = sem("ones_ready")
        low_scaled_ready = sem("low_scaled_ready")
        moe_split_ready = sem("moe_split_ready")
        expb_ready = sem("expb_ready")
        woT_lo_ready = sem("woT_lo_ready")
        G_sum_ready = sem("G_sum_ready")
        G_lo_ready = sem("G_lo_ready")
        Bf_lo_ready = sem("Bf_lo_ready")
        woG_lo_ready = sem("woG_lo_ready")
        y_bias_ready = sem("y_bias_ready")
        xT_lo_ready = sem("xT_lo_ready")
        hl_x_ready = sem("hl_x_ready")
        wqkv_ready = sem("wqkv_ready")
        sum_ready = sem("sum_ready")
        w_eff_lo1_ready = sem("w_eff_lo1_ready")
        stored = sem("stored")

        block = ctx.enter_context(nc.Block())

        @block.sync
        def _(sp):
            def load(name, dst, src):
                sp.dma_start(dst, src).then_inc(loaded[name], 16)

            def load_proj_weights(o):
                load(f"q{o}", q_i[:, o, :], q_t[:, o, :])
                load(f"moe{o}", moe[:, o, :], moe_w[:, o, :])

            load("lora_b", lora[:, 0, :], lora_in[:, 0, :])
            load("lora_a", lora[:, 1, :], lora_in[:, 1, :])
            load("small", small[:, :], small_in)
            load("hlT", hlT[:, :, :], hl_t)
            load("x_first", xT[:, 0, :, 0:SEQ], x_t[0, :, :, 0:SEQ])
            load_proj_weights(0)
            load("x_second", xT[:, 0, :, SEQ:PT], x_t[0, :, :, SEQ:PT])
            load("cond_w0", cond_n[:, 0:2, :], cond_w[:, 0:2, :])
            load_proj_weights(1)
            load("x1", xT[:, 1, :, :], x_t[1])
            load("cond_w1", cond_n[:, 2:4, :], cond_w[:, 2:4, :])
            load_proj_weights(2)
            load_proj_weights(3)
            load("woT", woT[:, :, :], wo_t)
            load("exp_b", expb[:, :, :], exp_b)
            load("x2", xT[:, 2:4, :, :].rearrange("p h t n -> p h (t n)"), x_t[2:4].rearrange("h p t n -> p h (t n)"))
            load("wqkv", wqkv_n[:, :, :], wqkv)
            load("ffn_bias", ffn_bias_bc[:, :], ffn_bias.partition_broadcast(P))
            load("lang", lang_i[:, :], lang.partition_broadcast(P))
            for b in range(BATCH - 1):
                sp.wait_ge(y_ready, b + 1)
                sp.dma_start(out[b], y_out[:, b, :]).then_inc(stored, 16)
            b = BATCH - 1
            for n in range(2):
                sp.wait_ge(y_ready, b + n + 1)
                s = slice(n * C // 2, (n + 1) * C // 2)
                sp.dma_start(out[b, :, s], y_out[:, b, s]).then_inc(stored, 16)
            sp.wait_ge(stored, 16 * (BATCH + 1))

        def g_block(ap, g):
            return ap[:, g // CT, (g % CT) * P:(g % CT + 1) * P]

        def x_pair(pair):
            return slice(pair * PT, (pair + 1) * PT)

        @block.scalar
        def _(act):
            def rounded(hi, full, ready):
                act.activation(hi, full, ACT.Copy).then_inc(ready, 1)

            act.wait_ge(loaded["lora_b"], 16)
            rounded(lora_bT[:, :], lora[:, 0, :], lora_b_hi_ready)
            act.wait_ge(loaded["lora_a"], 16)
            rounded(lora_a_hi[:, :], lora[:, 1, :], lora_a_hi_ready)
            act.wait_ge(loaded["small"], 16)
            act.activation(scale, scale, ACT.Exp).then_inc(scale_ready, 1)

            def moe_hi(o):
                act.wait_ge(loaded[f"moe{o}"], 16)
                rounded(split_a_hi[:, o, :], moe[:, o, :], moe_hi_ready)

            def normalise(h):
                act.wait_ge(wd_ready, h + 1)
                for g in range(h * GROUPS // 2, (h + 1) * GROUPS // 2):
                    act.activation(g_block(cond_n, g), g_block(cond_n, g), ACT.Copy, scale=inv_scale[:, g:g + 1])\
                       .then_inc(norm_ready, 1)

            def x_hi(pair):
                act.wait_ge(loaded[X_LOADS[2 * pair]], 16)
                act.wait_ge(loaded[X_LOADS[2 * pair + 1]], 16)
                rounded(xT_hi[:, :, x_pair(pair)], xT[:, pair, :, :], xT_hi_ready)

            def hl_raw(part, bank):
                ts = HL_PARTS[part]
                act.wait_ge(xhl_done, part + 1)
                act.activation(hl[:, ts[0]:ts[-1] + 1, :],
                               psum[bank][:, 0:len(ts) * HL].rearrange("p (t n) -> p t n", t=len(ts)),
                               ACT.Copy).then_inc(hl_raw_ready, 1)

            def delta_low(o):
                act.wait_ge(wd_ready, HALVES)
                act.wait_ge(low_scaled_ready, 1)
                for g in range(CT * o, CT * (o + 1)):
                    act.activation(g_block(delta, g), g_block(delta, g), ACT.Identity, bias=low_scaled[:, g:g + 1])\
                       .then_inc(delta_low_ready, 1)

            def delta_out(o):
                act.wait_ge(delta_done, o + 1)
                act.activation(delta[:, o, :], psum[o][:, :], ACT.Copy, scale=LORA_SCALE).then_inc(delta_ready, 1)

            def q_hi(o):
                act.wait_ge(loaded[f"q{o}"], 16)
                act.wait_ge(minus_zero_ready, 1)
                act.activation(split_b_hi[:, o, :], q_i[:, o, :], ACT.Identity, bias=minus_zero[:, :])\
                   .then_inc(qmz_hi_ready, 1)

            delta_out(0)
            moe_hi(0)
            delta_out(1)
            delta_out(2)
            delta_out(3)
            hl_raw(0, 4)
            q_hi(1)
            moe_hi(1)
            x_hi(0)
            x_hi(1)
            q_hi(2)
            moe_hi(2)
            q_hi(3)
            moe_hi(3)
            normalise(1)
            act.wait_ge(loaded["exp_b"], 16)
            rounded(expb_hi[:, :, :], expb[:, :, :], expb_hi_ready)
            act.wait_ge(loaded["woT"], 16)
            rounded(woT_hi, woT[:, :, :], woT_hi_ready)
            hl_raw(1, 5)

            def G_round(i):
                act.wait_ge(G_sum_ready, i + 1)
                rounded(G_hi[:, i, :], moe[:, i, :], G_hi_ready)

            act.wait_ge(moe_split_ready, CT)
            for i in range(CT):
                act.wait_ge(G_done, i + 1)
                act.activation(moe[:, i, :], psum[i][:, :], ACT.Copy, scale=ffn_scal).then_inc(G_ready, 1)
                if i >= 1:
                    G_round(i - 1)
            act.wait_ge(woHL_done, 1)
            act.activation(woHL[:, :], psum[6][:, 0:HL], ACT.Copy).then_inc(woHL_ready, 1)
            G_round(CT - 1)
            act.wait_ge(Bf_done, 1)
            act.wait_ge(ffn_scal2_ready, 1)
            act.activation(Bf, psum[7][:, :], ACT.Copy, scale=ffn_scal2[:, :]).then_inc(Bf_ready, 1)
            act.wait_ge(Bf_ready, 1)
            rounded(Bf_hi[:, :], Bf, Bf_ready)
            delta_low(0)
            hl_raw(2, 1)
            act.wait_ge(loaded["wqkv"], 16)
            for o in range(CT):
                rounded(wqkv_hi[:, o, :], wqkv_n[:, o, :], wqkv_hi_ready)
            act.wait_ge(woG_done, 1)
            act.activation(woG, psum[5][:, :], ACT.Copy).then_inc(woG_ready, 1)
            act.wait_ge(woG_ready, 1)
            rounded(woG_hi, woG, woG_ready)
            delta_low(1)
            act.wait_ge(minus_cut_ready, 1)
            act.activation(above, cond_n[:, 2:4, :], ACT.Sign, bias=minus_cut[:, :]).then_inc(above_ready, 1)
            act.wait_ge(above_ready, 1)
            act.activation(above, above, ACT.Relu).then_inc(above_ready, 1)

            def w_eff_hi(o):
                act.wait_ge(w_eff_ready, o + 1)
                rounded(split_a_hi[:, o, :], acc[:, o, :], w_eff_hi_ready)

            delta_low(2)
            w_eff_hi(0)
            delta_low(3)
            for o in range(1, CT):
                w_eff_hi(o)
            x_hi(2)
            x_hi(3)
            for i in range(CT):
                act.wait_ge(M_done, i + 1)
                act.activation(split_b_hi[:, i, 0:3 * D], psum[i][:, 0:3 * D], ACT.Copy).then_inc(M_hi_ready, 1)

            def qkv_out(h, which, bank, n):
                act.wait_ge(qkvT_done, n)
                if which == 2:
                    act.activation(vT[:, h, :], psum[bank][:, :], ACT.Copy).then_inc(qkvT_ready, 1)
                else:
                    act.activation((qT, kT)[which][:, h, :], psum[bank][:, :], ACT.Identity,
                                   bias=qkv_bias[:, which:which + 1]).then_inc(qkvT_ready, 1)

            def v_out(h, bank):
                act.wait_ge(v_done, h + 1)
                act.activation(v[:, h, :], psum[bank][:, :], ACT.Copy).then_inc(v_ready, 1)

            def exps(h, bank):
                act.wait_ge(max_ready, h + 1)
                for b in range(TPH):
                    n = TPH * h + b
                    act.activation(probs[:, h, b * P:(b + 1) * P], psum[bank][:, b * P:(b + 1) * P], ACT.Exp,
                                   bias=neg_max[:, n:n + 1], scale=SOFTMAX_SCALE,
                                   accum_out=row_sum[:, n:n + 1]).then_inc(exp_ready, 1)

            def probsT_out(h, bank):
                act.wait_ge(probsT_done, h + 1)
                act.activation(probsT[:, h, :], psum[bank][:, :], ACT.Copy).then_inc(probsT_ready, 1)

            def oT_out(h, bank):
                act.wait_ge(oT_done, h + 1)
                act.activation(oT[:, h, :], psum[bank][:, :], ACT.Identity, bias=qkv_bias[:, 2:3])\
                   .then_inc(oT_ready, 1)
                act.wait_ge(oT_ready, h + 1)
                act.activation(oT_hi[:, h, :], oT[:, h, :], ACT.Copy).then_inc(oT_hi_ready, 1)

            def top_exps(h):
                act.wait_ge(top_diff_ready, h + 1)
                act.activation(top_exp[:, TPH * h:TPH * (h + 1)], top_exp[:, TPH * h:TPH * (h + 1)], ACT.Exp)\
                   .then_inc(top_exp_ready, 1)

            def ghT_out(h, bank):
                act.wait_ge(ghT_done, h + 1)
                act.activation(ghT_hi[:, h, :], psum[bank][:, :], ACT.Copy).then_inc(ghT_hi_ready, 1)

            qkv_out(0, 0, 0, 1)
            qkv_out(0, 1, 1, 2)
            qkv_out(0, 2, 2, 3)
            act.wait_ge(boHL_done, 1)
            act.activation(hl_bias[:, :], psum[1][:, 0:HL], ACT.Copy).then_inc(hl_bias_ready, 1)
            exps(0, 3)
            qkv_out(1, 2, 0, 4)
            v_out(0, 2)
            act.wait_ge(boG_done, 1)
            act.activation(boG, psum[1][:, :], ACT.Copy).then_inc(boG_ready, 1)
            probsT_out(0, 3)
            qkv_out(1, 1, 2, 5)
            oT_out(0, 0)
            qkv_out(1, 0, 3, 6)
            top_exps(0)
            ghT_out(0, 1)
            exps(1, 0)
            v_out(1, 2)
            hl_raw(3, 3)
            probsT_out(1, 0)
            oT_out(1, 1)
            top_exps(1)
            ghT_out(1, 0)

        @block.gpsimd
        def _(pool):
            steps = [0]

            def alone(ins):
                steps[0] += 1
                ins.then_inc(pool_step, 1)
                pool.wait_ge(pool_step, steps[0])

            def rest(lo, full, hi, ready):
                pool.tensor_tensor(lo, full, hi, ALU.subtract).then_inc(ready, 1)

            alone(pool.memset(ident[:, :], 0.0))
            pool.affine_select(out=ident[:, :], in_=ident[:, :], compare_op=ALU.not_equal, fill=1.0,
                               base=0, pattern=[[-1, P]], channel_multiplier=1).then_inc(ident_ready, 1)
            pool.memset(ones[:, :], 1.0).then_inc(ones_ready, 1)
            for e in range(E):
                pool.memset(expert_no[:, e:e + 1], float(e)).then_inc(ident_ready, 1)

            def x_lo(pair):
                pool.wait_ge(xT_hi_ready, pair + 1)
                rest(xT_lo[:, :, x_pair(pair)], xT[:, pair, :, :], xT_hi[:, :, x_pair(pair)], xT_lo_ready)

            for o in range(CT):
                pool.wait_ge(moe_hi_ready, o + 1)
                rest(split_a_lo[:, o, :], moe[:, o, :], split_a_hi[:, o, :], moe_split_ready)
                if o == 1:
                    x_lo(0)
            pool.wait_ge(scale_ready, 1)
            pool.wait_ge(levels_ready, 1)
            pool.tensor_tensor(low_scaled[:, :], scale, levels[:, 0:1].to_broadcast([P, GROUPS]), ALU.mult)\
                .then_inc(low_scaled_ready, 1)
            pool.wait_ge(expb_hi_ready, 1)
            rest(expb_lo[:, :, :], expb[:, :, :], expb_hi[:, :, :], expb_ready)
            pool.wait_ge(woT_hi_ready, 1)
            pool.wait_ge(delta_ready, CT)
            rest(woT_lo, woT[:, :, :], woT_hi, woT_lo_ready)
            for i in range(CT):
                pool.wait_ge(G_ready, i + 1)
                d = moe[:, i, i * P:(i + 1) * P]
                pool.tensor_tensor(d, d, ident[:, :], ALU.add).then_inc(G_sum_ready, 1)
                if i >= 1:
                    pool.wait_ge(G_hi_ready, i)
                    rest(G_lo[:, i - 1, :], moe[:, i - 1, :], G_hi[:, i - 1, :], G_lo_ready)
            pool.wait_ge(G_hi_ready, CT)
            rest(G_lo[:, CT - 1, :], moe[:, CT - 1, :], G_hi[:, CT - 1, :], G_lo_ready)
            x_lo(1)

            def wqkv_rest(o):
                pool.wait_ge(wqkv_hi_ready, o + 1)
                rest(wqkv_lo[:, o, :], wqkv_n[:, o, :], wqkv_hi[:, o, :], wqkv_ready)

            def cut_sum(n):
                pool.wait_ge(step_ready, n)
                pool.tensor_tensor(acc[:, 2:4, :], acc[:, 2:4, :], step[:, 2:4, :], ALU.add).then_inc(sum_ready, 1)

            cut_sum(1)
            wqkv_rest(0)
            pool.wait_ge(sum_ready, 1)
            cut_sum(2)
            wqkv_rest(1)
            wqkv_rest(2)
            pool.wait_ge(w_eff_hi_ready, 2)
            rest(split_a_lo[:, 1, :], acc[:, 1, :], split_a_hi[:, 1, :], w_eff_lo1_ready)
            wqkv_rest(3)
            x_lo(2)
            x_lo(3)
            pool.wait_ge(woG_ready, 2)
            rest(woG_lo, woG, woG_hi, woG_lo_ready)

            def hl_x(part):
                ts = HL_PARTS[part]
                t = slice(ts[0], ts[-1] + 1)
                pool.wait_ge(hl_raw_ready, part + 1)
                pool.wait_ge(hl_bias_ready, 1)
                alone(pool.tensor_tensor(hl[:, t, :], hl[:, t, :],
                                         hl_bias[:, :].unsqueeze(1).to_broadcast([P, len(ts), HL]), ALU.add))
                pool.wait_ge(lang_hot_ready, 1)
                pool.tensor_tensor(hl[:, t, ER:HL], hl[:, t, ER:HL], lang_hot[:, t, :], ALU.add)\
                    .then_inc(hl_x_ready, 1)

            hl_x(0)
            hl_x(1)
            pool.wait_ge(Bf_ready, 2)
            rest(Bf_lo[:, :], Bf, Bf_hi[:, :], Bf_lo_ready)
            hl_x(2)
            pool.wait_ge(boG_ready, 1)
            pool.wait_ge(loaded["ffn_bias"], 16)
            pool.tensor_tensor(y_bias[:, :], boG, ffn_bias_bc[:, :], ALU.add).then_inc(y_bias_ready, 1)
            hl_x(3)

        @block.vector
        def _(dve):
            steps = [0]

            def mark(ins):
                steps[0] += 1
                ins.then_inc(dve_step, 1)
                return steps[0]

            def alone(ins):
                dve.wait_ge(dve_step, mark(ins))

            dve.wait_ge(lora_b_hi_ready, 1)
            dve.tensor_tensor(lora_bT[RANK:P, :], lora[RANK:P, 0, :], lora_bT[RANK:P, :], ALU.subtract)\
               .then_inc(lora_lo_ready, 1)
            dve.wait_ge(lora_a_hi_ready, 1)
            dve.tensor_tensor(lora_a_lo[:, :], lora[:, 1, :], lora_a_hi[:, :], ALU.subtract).then_inc(lora_lo_ready, 1)

            dve.wait_ge(loaded["small"], 16)
            dve.tensor_scalar(ffn_scal2[:, :], ffn_scal, EXPERT_SCALE, None, ALU.mult).then_inc(ffn_scal2_ready, 1)
            dve.tensor_scalar(minus_zero[:, :], zero_point, -1.0, None, ALU.mult).then_inc(minus_zero_ready, 1)
            mark(dve.tensor_reduce(cb_tmp[:, 0:1], cb, AX.X, ALU.max))
            alone(dve.tensor_reduce(cb_tmp[:, 1:2], cb, AX.X, ALU.min))
            one = mark(dve.tensor_scalar(cb_tmp[:, 1:2], cb_tmp[:, 1:2], -1.0, CODEBOOK_FLOOR, ALU.mult, ALU.max))
            dve.wait_ge(loaded["hlT"], 16)
            bo_at = mark(dve.tensor_scalar(bo_HL[:, :], hlT[:, 0, :], bo_col[:, 0:1], None, ALU.mult))
            dve.wait_ge(dve_step, one)
            one = mark(dve.tensor_tensor(cb_tmp[:, 2:3], cb_tmp[:, 0:1], cb_tmp[:, 1:2], ALU.max))

            def bo_hl_step(c):
                dve.wait_ge(dve_step, bo_at)
                return mark(dve.scalar_tensor_tensor(bo_HL[:, :], hlT[:, c, :], bo_col[:, c:c + 1], bo_HL[:, :],
                                                     ALU.mult, ALU.add))

            bo_at = bo_hl_step(1)
            dve.wait_ge(dve_step, one)
            one = mark(dve.reciprocal(cb_tmp[:, 3:4], cb_tmp[:, 2:3]))
            bo_at = bo_hl_step(2)
            dve.wait_ge(dve_step, one)
            dve.tensor_scalar(levels[:, :], cb, cb_tmp[:, 3:4], None, ALU.mult).then_inc(levels_ready, 1)
            dve.wait_ge(dve_step, bo_at)
            dve.scalar_tensor_tensor(bo_HL[:, :], hlT[:, CT - 1, :], bo_col[:, CT - 1:CT], bo_HL[:, :],
                                     ALU.mult, ALU.add).then_inc(bo_HL_ready, 1)
            dve.wait_ge(levels_ready, 1)
            dve.tensor_tensor(rises[:, :], levels[:, 1:LEVELS], levels[:, 0:CUTS], ALU.subtract).then_inc(rises_ready, 1)
            alone(dve.tensor_tensor(cuts[:, :], levels[:, 1:LEVELS], levels[:, 0:CUTS], ALU.add))
            cuts_at = mark(dve.tensor_scalar(cuts[:, :], cuts[:, :], 0.5, None, ALU.mult))
            dve.wait_ge(scale_ready, 1)
            dve.reciprocal(inv_scale[:, :], scale).then_inc(inv_scale_ready, 1)

            def keep(j, op, k):
                return mark(dve.tensor_tensor(cuts[:, j:j + 1], cuts[:, j:j + 1], cuts[:, k:k + 1], op))

            def qmz(o):
                if o == 0:
                    dve.wait_ge(loaded["q0"], 16)
                    dve.wait_ge(dve_step, mark(dve.tensor_scalar(split_b_hi[:, o, :], q_i[:, o, :], zero_point, None,
                                                                 ALU.subtract)))
                else:
                    dve.wait_ge(qmz_hi_ready, o)
                dve.scalar_tensor_tensor(split_b_lo[:, o, :], q_i[:, o, :], zero_point, split_b_hi[:, o, :],
                                         ALU.subtract, ALU.subtract).then_inc(qmz_ready, 1)

            def w_delta(h):
                t = slice(2 * h, 2 * h + 2)
                dve.wait_ge(loaded[f"cond_w{h}"], 16)
                dve.wait_ge(delta_ready, 2 * (h + 1))
                dve.tensor_tensor(cond_n[:, t, :], cond_n[:, t, :], delta[:, t, :], ALU.add).then_inc(wd_ready, 1)

            def half(ap, h):
                return ap[:, 2 * h:2 * h + 2, :].rearrange("p t n -> p (t n)")

            def blocks(h):
                return cond_n[:, 2 * h:2 * h + 2, :].rearrange("p t (g n) -> p (t g) n", n=P)

            made, added = {}, {}

            def cut_at(j, h):
                if j == 0 and h == 0:
                    dve.wait_ge(norm_half_ready, 1)
                elif j == 0:
                    dve.wait_ge(norm_ready, GROUPS // 2)
                elif (j, h) == (CUTS - 2, 1):
                    dve.wait_ge(sum_ready, 1)
                elif j >= 2:
                    dve.wait_ge(dve_step, added[h])
                dst = acc if j == 0 else step
                ins = dve.tensor_scalar(half(dst, h), half(cond_n, h), cuts[:, j:j + 1], rises[:, j:j + 1],
                                        ALU.is_gt, ALU.mult)
                if h == 1 and j in (CUTS - 3, CUTS - 2):
                    ins.then_inc(step_ready, 1)
                else:
                    made[h] = mark(ins)

            def cut_add(h):
                dve.wait_ge(dve_step, made[h])
                added[h] = mark(dve.tensor_tensor(half(acc, h), half(acc, h), half(step, h), ALU.add))

            qmz(0)
            w_delta(0)
            dve.wait_ge(dve_step, cuts_at)
            keep(1, ALU.min, 3)
            keep(5, ALU.max, 3)
            kept = keep(4, ALU.max, 3)
            dve.wait_ge(wd_ready, 1)
            dve.wait_ge(inv_scale_ready, 1)
            dve.tensor_tensor(blocks(0), blocks(0), inv_scale[:, 0:GROUPS // 2].unsqueeze(2).to_broadcast(
                [P, GROUPS // 2, P]), ALU.mult).then_inc(norm_half_ready, 1)
            dve.wait_ge(dve_step, kept)
            keep(0, ALU.min, 1)
            keep(2, ALU.max, 1)
            keep(4, ALU.min, 5)
            kept = keep(6, ALU.max, 5)
            dve.wait_ge(rises_ready, 1)
            qmz(1)
            dve.wait_ge(dve_step, kept)
            cut_at(0, 0)
            cut_at(1, 0)
            w_delta(1)
            qmz(2)
            dve.wait_ge(dve_step, kept)
            kept = keep(2, ALU.min, 3)
            cut_add(0)
            qmz(3)
            dve.wait_ge(dve_step, kept)
            dve.tensor_scalar(minus_cut[:, :], cuts[:, CUTS - 1:CUTS], -1.0, None, ALU.mult).then_inc(minus_cut_ready, 1)
            cut_at(2, 0)
            cut_add(0)
            cut_at(0, 1)
            cut_at(1, 1)
            cut_add(1)
            cut_at(3, 0)
            cut_at(2, 1)
            cut_add(0)
            cut_add(1)
            cut_at(4, 0)
            cut_at(3, 1)
            cut_add(0)
            cut_add(1)
            cut_at(5, 0)
            cut_at(4, 1)
            cut_add(0)
            cut_at(6, 0)
            cut_at(5, 1)
            cut_add(0)

            def w_eff(o):
                dve.wait_ge(dve_step, added[o // 2])
                for g in range(CT * o, CT * (o + 1)):
                    dve.wait_ge(delta_low_ready, g + 1)
                    ins = dve.scalar_tensor_tensor(g_block(acc, g), g_block(acc, g), scale[:, g:g + 1],
                                                   g_block(delta, g), ALU.mult, ALU.add)
                ins.then_inc(w_eff_ready, 1)

            def w_eff_lo(o):
                dve.wait_ge(w_eff_hi_ready, o + 1)
                dve.tensor_tensor(split_a_lo[:, o, :], acc[:, o, :], split_a_hi[:, o, :], ALU.subtract)\
                   .then_inc(w_eff_lo_ready, 1)

            w_eff(0)
            w_eff(1)
            w_eff_lo(0)
            dve.wait_ge(sum_ready, 2)
            dve.wait_ge(above_ready, 2)
            added[1] = mark(dve.scalar_tensor_tensor(half(acc, 1), above.rearrange("p t n -> p (t n)"),
                                                     rises[:, CUTS - 1:CUTS], half(acc, 1), ALU.mult, ALU.add))
            w_eff(2)
            w_eff(3)
            w_eff_lo(2)
            w_eff_lo(3)
            for i in range(CT):
                dve.wait_ge(M_hi_ready, i + 1)
                dve.tensor_tensor(split_b_lo[:, i, 0:3 * D], psum[i][:, 0:3 * D], split_b_hi[:, i, 0:3 * D],
                                  ALU.subtract).then_inc(M_lo_ready, 1)

            dve.wait_ge(loaded["lang"], 16)
            alone(dve.tensor_copy(lang_f[:, :], lang_i[:, :]))
            dve.wait_ge(ident_ready, 1 + E)
            alone(dve.tensor_tensor(lang_hot[:, :, :], lang_f[:, :].unsqueeze(2).to_broadcast([P, BATCH, E]),
                                    expert_no[:, :].unsqueeze(1).to_broadcast([P, BATCH, E]), ALU.is_equal))
            dve.tensor_scalar(lang_hot[:, :, :], lang_hot[:, :, :], LANG_BIAS, None, ALU.mult).then_inc(lang_hot_ready, 1)

            dve.wait_ge(G_sum_ready, CT)
            one = mark(dve.tensor_scalar(bo_G[:, :], moe[:, 0, :], bo_col[:, 0:1], None, ALU.mult))
            for c in range(1, CT):
                dve.wait_ge(dve_step, one)
                one = mark(dve.scalar_tensor_tensor(bo_G[:, :], moe[:, c, :], bo_col[:, c:c + 1], bo_G[:, :],
                                                    ALU.mult, ALU.add))
            dve.wait_ge(ones_ready, 1)
            mark(dve.tensor_copy(ones_r[:, :], ones[:, :]))
            dve.wait_ge(dve_step, one)
            dve.tensor_copy(bo_G_hi[:, :], bo_G[:, :]).then_inc(bo_G_ready, 1)
            dve.wait_ge(bo_G_ready, 1)
            dve.tensor_tensor(bo_G_lo[:, :], bo_G[:, :], bo_G_hi[:, :], ALU.subtract).then_inc(bo_G_ready, 1)

            def softmax_max(h, bank):
                dve.wait_ge(scores_done, h + 1)
                m = neg_max[:, TPH * h:TPH * (h + 1)]
                alone(dve.tensor_reduce(m, psum[bank][:, :].rearrange("p (b k) -> p b k", b=TPH), AX.X, ALU.max))
                dve.tensor_scalar(m, m, -SOFTMAX_SCALE, None, ALU.mult).then_inc(max_ready, 1)

            def softmax_norm(h):
                dve.wait_ge(exp_ready, TPH * (h + 1))
                s = row_sum[:, TPH * h:TPH * (h + 1)]
                alone(dve.reciprocal(s, s))
                pr = probs[:, h, :].rearrange("p (b k) -> p b k", b=TPH)
                dve.tensor_tensor(pr, pr, s.unsqueeze(2).to_broadcast([P, TPH, P]), ALU.mult).then_inc(probs_ready, 1)

            def o_lo(h):
                dve.wait_ge(oT_hi_ready, h + 1)
                dve.tensor_tensor(oT_lo[:, h, :], oT[:, h, :], oT_hi[:, h, :], ALU.subtract).then_inc(oT_lo_ready, 1)

            def gating(h, banks):
                t0 = TPH * h
                T = slice(t0, t0 + TPH)

                def add_o(pair, cols):
                    p = hl[:, t0 + 2 * pair:t0 + 2 * pair + 2, cols]
                    o = psum[banks[pair]][:, 0:2 * HL].rearrange("p (t n) -> p t n", t=2)[:, :, cols]
                    return dve.tensor_tensor(p, o, p, ALU.add)

                for pair in range(2):
                    dve.wait_ge(hl_done, 2 * h + pair + 1)
                    dve.wait_ge(hl_x_ready, pair + 1 if h == 0 else len(HL_PARTS))
                    add_o(pair, slice(ER, HL)).then_inc(logits_ready, 1)
                for t in range(t0, t0 + TPH):
                    dve.wait_ge(logits_ready, 2 * h + (t - t0) // 2 + 1)
                    last = mark(dve.max(top[:, t, :], hl[:, t, ER:HL]))
                dve.wait_ge(dve_step, last)
                dve.tensor_tensor(top_exp[:, T], top[:, T, 1], top[:, T, 0], ALU.subtract).then_inc(top_diff_ready, 1)
                for t in range(t0, t0 + TPH):
                    last = mark(dve.max_index(top_at[:, t, :], top[:, t, :], hl[:, t, ER:HL]))
                add_o(0, slice(0, ER)).then_inc(hl_read, 1)
                dve.wait_ge(dve_step, last)
                nos = expert_no[:, :].unsqueeze(1).to_broadcast([P, TPH, E])

                def over_experts(ap):
                    return ap.unsqueeze(2).to_broadcast([P, TPH, E])

                mark(dve.tensor_tensor(gate[:, T, :], nos, over_experts(top_at[:, T, 0]), ALU.is_equal))
                hot = mark(dve.tensor_tensor(gate2[:, T, :], nos, over_experts(top_at[:, T, 1]), ALU.is_equal))
                add_o(1, slice(0, ER)).then_inc(hl_read, 1)
                dve.wait_ge(top_exp_ready, h + 1)
                dve.wait_ge(dve_step, hot)
                one = mark(dve.tensor_tensor(gate2[:, T, :], gate2[:, T, :], over_experts(top_exp[:, T]), ALU.mult))
                both = mark(dve.tensor_scalar(weight[:, T], top_exp[:, T], 1.0, None, ALU.add))
                dve.wait_ge(dve_step, one)
                mark(dve.tensor_tensor(gate[:, T, :], gate[:, T, :], gate2[:, T, :], ALU.add))
                dve.wait_ge(dve_step, both)
                alone(dve.reciprocal(weight[:, T], weight[:, T]))
                alone(dve.tensor_tensor(gate[:, T, :], gate[:, T, :], over_experts(weight[:, T]), ALU.mult))
                dve.wait_ge(hl_read, 2 * h + 2)
                dve.tensor_tensor(gh[:, h, :].rearrange("p (t e r) -> p t e r", t=TPH, e=E),
                                  hl[:, T, 0:ER].rearrange("p t (e r) -> p t e r", e=E),
                                  gate[:, T, :].unsqueeze(3).to_broadcast([P, TPH, E, R]), ALU.mult)\
                   .then_inc(gh_ready, 1)

            def gh_lo(h, bank):
                dve.wait_ge(ghT_hi_ready, h + 1)
                dve.tensor_tensor(ghT_lo[:, h, :], psum[bank][:, :], ghT_hi[:, h, :], ALU.subtract)\
                   .then_inc(ghT_lo_ready, 1)

            def y_store(t, n=slice(0, C)):
                dve.wait_ge(y_done, t + 1)
                dve.wait_ge(y_bias_ready, 1)
                dve.tensor_tensor(y_out[:, t, n], psum[4 + t % 4][:, n], y_bias[:, n], ALU.add).then_inc(y_ready, 1)

            softmax_max(0, 3)
            softmax_norm(0)
            o_lo(0)
            gating(0, (1, 2))
            softmax_max(1, 0)
            gh_lo(0, 1)
            softmax_norm(1)
            dve.wait_ge(w_eff_lo1_ready, 1)
            for t in range(TPH):
                y_store(t)
            o_lo(1)
            gating(1, (2, 3))
            gh_lo(1, 0)
            for t in range(TPH, BATCH - 1):
                y_store(t)
            for n in range(2):
                y_store(BATCH - 1, slice(n * C // 2, (n + 1) * C // 2))

        @block.tensor
        def _(pe):
            def three(out_ap, l_hi, l_lo, r_hi, r_lo, first, last):
                pe.matmul(out_ap, l_hi, r_hi, start=first, stop=False)
                pe.matmul(out_ap, l_hi, r_lo, start=False, stop=False)
                return pe.matmul(out_ap, l_lo, r_hi, start=False, stop=last)

            pe.wait_ge(ident_ready, 1)
            for _ in range(WARM_UP):
                pe.transpose(psum[7][:, 0:P], ident[:, :], ident[:, :])

            pe.wait_ge(lora_lo_ready, 2)
            for o in range(CT):
                pe.matmul(psum[o][:, :], lora_bT[:, o * P:(o + 1) * P], lora_a_hi[:, :], start=True, stop=False)
                pe.matmul(psum[o][:, :], lora_bT[:, o * P:(o + 1) * P], lora_a_lo[:, :], start=False, stop=True)\
                  .then_inc(delta_done, 1)

            def x_hl(part, bank, batches=None):
                for t in (batches or HL_PARTS[part]):
                    pe.wait_ge(loaded[X_LOADS[t]], 16)
                    at, s = (t - HL_PARTS[part][0]) * HL, slice(t % 2 * SEQ, (t % 2 + 1) * SEQ)
                    for c in range(CT):
                        mm = pe.matmul(psum[bank][:, at:at + HL], xT[:, t // 2, c, s], hlT[:, c, :],
                                       start=(c == 0), stop=(c == CT - 1))
                if t == HL_PARTS[part][-1]:
                    mm.then_inc(xhl_done, 1)

            def G_product(o):
                pe.wait_ge(qmz_ready, o + 1)
                pe.wait_ge(moe_split_ready, o + 1)
                for i in range(CT):
                    s = slice(i * P, (i + 1) * P)
                    if o == 0:
                        pe.wait_ge(delta_ready, i + 1)
                    mm = three(psum[i][:, :], split_a_hi[:, o, s], split_a_lo[:, o, s],
                               split_b_hi[:, o, :], split_b_lo[:, o, :], o == 0, o == CT - 1)
                    if o == CT - 1:
                        mm.then_inc(G_done, 1)

            pe.wait_ge(loaded["hlT"], 16)
            x_hl(0, 4)
            G_product(0)
            x_hl(1, 5)
            G_product(1)
            G_product(2)
            G_product(3)
            pe.wait_ge(loaded["woT"], 16)
            for c in range(CT):
                mm = pe.matmul(psum[6][:, 0:HL], woT[:, c, :], hlT[:, c, :], start=(c == 0), stop=(c == CT - 1))
            mm.then_inc(woHL_done, 1)
            pe.wait_ge(expb_ready, 1)
            for o in range(CT):
                mm = three(psum[7][:, :], expb_hi[:, o, :], expb_lo[:, o, :], split_b_hi[:, o, :],
                           split_b_lo[:, o, :], o == 0, o == CT - 1)
            mm.then_inc(Bf_done, 1)
            pe.wait_ge(G_ready, 2)
            x_hl(2, 1)

            def y_x(t, channels=range(CT)):
                for c in channels:
                    s = slice(t * SEQ, (t + 1) * SEQ)
                    three(psum[4 + t % 4][:, :], xT_hi[:, c, s], xT_lo[:, c, s], G_hi[:, c, :], G_lo[:, c, :],
                          c == 0, False)

            def y_o(t):
                h, s = t // TPH, slice((t % TPH) * SEQ, (t % TPH + 1) * SEQ)
                three(psum[4 + t % 4][:, :], oT_hi[:, h, s], oT_lo[:, h, s], woG_hi, woG_lo, False, False)

            def y_gh(t):
                h, s = t // TPH, slice((t % TPH) * SEQ, (t % TPH + 1) * SEQ)
                three(psum[4 + t % 4][:, :], ghT_hi[:, h, s], ghT_lo[:, h, s], Bf_hi[:, :], Bf_lo[:, :], False, True)\
                    .then_inc(y_done, 1)

            pe.wait_ge(woT_lo_ready, 1)
            pe.wait_ge(hl_raw_ready, 2)
            for c in range(CT):
                pe.wait_ge(G_hi_ready, c + 1)
                pe.wait_ge(G_lo_ready, c + 1)
                mm = three(psum[5][:, :], woT_hi[:, c, :], woT_lo[:, c, :], G_hi[:, c, :], G_lo[:, c, :],
                           c == 0, c == CT - 1)
                if c == CT - 1:
                    mm.then_inc(woG_done, 1)
                if c == 0:
                    pe.wait_ge(xT_lo_ready, 1)
                y_x(0, range(c, c + 1))
            pe.wait_ge(xT_lo_ready, 2)
            pe.wait_ge(woHL_ready, 1)
            y_x(2)
            pe.wait_ge(woG_ready, 1)
            y_x(1)
            pe.wait_ge(Bf_ready, 1)
            y_x(3)

            pe.wait_ge(hl_raw_ready, 3)
            for o in range(CT):
                pe.wait_ge(wqkv_ready, o + 1)
                if o == 1:
                    pe.wait_ge(w_eff_lo1_ready, 1)
                else:
                    pe.wait_ge(w_eff_lo_ready, max(1, o))
                for i in range(CT):
                    s = slice(i * P, (i + 1) * P)
                    mm = three(psum[i][:, 0:3 * D], split_a_hi[:, o, s], split_a_lo[:, o, s], wqkv_hi[:, o, :],
                               wqkv_lo[:, o, :], o == 0, o == CT - 1)
                    if o == CT - 1:
                        mm.then_inc(M_done, 1)

            def qkv(h, which, bank):
                for i in range(CT):
                    if (h, which) == (0, 0):
                        pe.wait_ge(M_lo_ready, i + 1)
                    m = slice(which * D, (which + 1) * D)
                    s = slice(h * HT, (h + 1) * HT)
                    mm = three(psum[bank][:, :], split_b_hi[:, i, m], split_b_lo[:, i, m], xT_hi[:, i, s],
                               xT_lo[:, i, s], i == 0, i == CT - 1)
                mm.then_inc(qkvT_done, 1)

            def v_rows(h, bank):
                for b in range(TPH):
                    mm = pe.transpose(psum[bank][:, b * P:(b + 1) * P], vT[:, h, b * P:(b + 1) * P], ident[:, :])
                mm.then_inc(v_done, 1)

            def scores(h, bank):
                for b in range(TPH):
                    s = slice(b * P, (b + 1) * P)
                    mm = pe.matmul(psum[bank][:, s], qT[:, h, s], kT[:, h, s], start=True, stop=True)
                mm.then_inc(scores_done, 1)

            def probs_turn(h, bank):
                pe.wait_ge(probs_ready, h + 1)
                for b in range(TPH):
                    s = slice(b * P, (b + 1) * P)
                    mm = pe.transpose(psum[bank][:, s], probs[:, h, s], ident[:, :])
                mm.then_inc(probsT_done, 1)

            def attend(h, bank):
                pe.wait_ge(probsT_ready, h + 1)
                pe.wait_ge(v_ready, h + 1)
                for b in range(TPH):
                    s = slice(b * P, (b + 1) * P)
                    mm = pe.matmul(psum[bank][:, s], v[:, h, s], probsT[:, h, s], start=True, stop=True)
                mm.then_inc(oT_done, 1)

            def o_hl(h, pair, bank):
                for t in range(2):
                    s = slice((2 * pair + t) * P, (2 * pair + t + 1) * P)
                    mm = pe.matmul(psum[bank][:, t * HL:(t + 1) * HL], oT[:, h, s], woHL[:, :], start=True, stop=True)
                mm.then_inc(hl_done, 1)

            def gh_turn(h, bank):
                pe.wait_ge(gh_ready, h + 1)
                for b in range(TPH):
                    s = slice(b * P, (b + 1) * P)
                    mm = pe.transpose(psum[bank][:, s], gh[:, h, s], ident[:, :])
                mm.then_inc(ghT_done, 1)

            qkv(0, 0, 0)
            qkv(0, 1, 1)
            qkv(0, 2, 2)
            pe.wait_ge(qkvT_ready, 2)
            scores(0, 3)
            pe.wait_ge(ones_ready, 1)
            pe.wait_ge(bo_HL_ready, 1)
            pe.matmul(psum[1][:, 0:HL], ones[:, :], bo_HL[:, :], start=True, stop=True).then_inc(boHL_done, 1)
            pe.wait_ge(xT_lo_ready, PAIRS)
            qkv(1, 2, 0)
            pe.wait_ge(qkvT_ready, 3)
            v_rows(0, 2)
            pe.wait_ge(hl_bias_ready, 1)
            pe.wait_ge(bo_G_ready, 2)
            pe.matmul(psum[1][:, :], ones_r[:, :], bo_G_hi[:, :], start=True, stop=False)
            pe.matmul(psum[1][:, :], ones_r[:, :], bo_G_lo[:, :], start=False, stop=True).then_inc(boG_done, 1)
            probs_turn(0, 3)
            pe.wait_ge(v_ready, 1)
            qkv(1, 1, 2)
            pe.wait_ge(qkvT_ready, 4)
            attend(0, 0)
            qkv(1, 0, 3)
            pe.wait_ge(oT_ready, 1)
            pe.wait_ge(woHL_ready, 1)
            pe.wait_ge(boG_ready, 1)
            o_hl(0, 0, 1)
            pe.wait_ge(qkvT_ready, 5)
            o_hl(0, 1, 2)
            pe.wait_ge(oT_hi_ready, 1)
            pe.wait_ge(oT_lo_ready, 1)
            pe.wait_ge(woG_lo_ready, 1)
            y_o(0)
            pe.wait_ge(qkvT_ready, 6)
            scores(1, 0)
            for t in range(1, TPH):
                y_o(t)
            x_hl(3, 3, (5,))
            gh_turn(0, 1)
            x_hl(3, 3, (6, 7))
            v_rows(1, 2)
            pe.wait_ge(ghT_hi_ready, 1)
            pe.wait_ge(ghT_lo_ready, 1)
            pe.wait_ge(Bf_lo_ready, 1)
            for t in range(TPH):
                y_gh(t)
            probs_turn(1, 0)
            pe.wait_ge(y_ready, 1)
            y_x(4)
            attend(1, 1)
            pe.wait_ge(y_ready, 2)
            y_x(5)
            pe.wait_ge(oT_ready, 2)
            o_hl(1, 0, 2)
            pe.wait_ge(hl_raw_ready, 4)
            o_hl(1, 1, 3)
            pe.wait_ge(oT_hi_ready, 2)
            pe.wait_ge(oT_lo_ready, 2)
            y_o(4)
            y_o(5)
            pe.wait_ge(y_ready, 3)
            y_x(6)
            y_o(6)
            gh_turn(1, 0)
            pe.wait_ge(y_ready, 4)
            y_x(7, range(0, CT - 1))
            pe.wait_ge(ghT_hi_ready, 2)
            pe.wait_ge(ghT_lo_ready, 2)
            for t in range(TPH, BATCH - 1):
                y_gh(t)
            y_x(7, range(CT - 1, CT))
            y_o(7)
            y_gh(7)



_INPUTS = ["small", "lora", "hl_t", "x_t", "cond_w", "q_t", "moe_w", "wo_t", "exp_b", "wqkv", "ffn_bias", "lang"]


def layouts(i):
    import numpy as np

    a = {n: np.asarray(v) for n, v in i.items()}

    def tiles(m):
        return m.reshape(-1, P, m.shape[-1]).transpose(1, 0, 2)

    def all_rows(v):
        return np.broadcast_to(v.reshape(1, -1), (P, v.size))

    def columns(v):
        return v.reshape(-1, P).T

    x = a["x"]
    n_exp, rank, ch = a["L0_cond2_A"].shape
    pairs = x.shape[0] // 2
    lora_bt, lora_a = a["L0_cond_lora_B"].T, a["L0_cond_lora_A"]
    laid = {
        "small": np.concatenate([all_rows(a["condB_codebook"]), all_rows(a["L0_ffn_scale"]),
                                 all_rows(a["L0_ffn_zero_point"]), columns(a["L0_attn_bqkv"]),
                                 columns(a["L0_attn_bo"]),
                                 tiles(a["L0_cond_scale_log"].reshape(ch, -1)).reshape(P, -1)], axis=1),
        "lora": np.stack([np.concatenate([lora_bt, lora_bt]), np.concatenate([lora_a, lora_a])], axis=1),
        "hl_t": tiles(np.concatenate([a["L0_cond2_A"].reshape(n_exp * rank, ch), a["L0_cond2_Wr"]]).T),
        "x_t": x.reshape(pairs, 2 * x.shape[1], ch // P, P).transpose(0, 3, 2, 1),
        "cond_w": tiles(a["L0_cond_weight"]),
        "q_t": tiles(a["L0_ffn_qweight"].T),
        "moe_w": tiles(a["L0_cond2_W"]),
        "wo_t": tiles(a["L0_attn_Wo"].T),
        "exp_b": tiles(a["L0_cond2_B"].transpose(1, 0, 2).reshape(ch, n_exp * rank)),
        "wqkv": tiles(a["L0_attn_Wqkv"]),
        "ffn_bias": a["L0_ffn_bias"],
        "lang": a["itok_B_0_7"],
    }
    return {n: np.ascontiguousarray(laid[n]) for n in _INPUTS}


def kernel(**inputs):
    import concourse.bacc as bacc
    from concourse.bass_utils import run_bass_kernel_spmd

    nc = bacc.Bacc("TRN2", target_bir_lowering=False, num_devices=1)
    arrays = layouts(inputs)
    args = [nc.dram_tensor("in_" + n, a.shape, mybir.dt.from_np(a.dtype), kind="ExternalInput").ap()
            for n, a in arrays.items()]
    out = nc.dram_tensor("out", inputs["x"].shape, F32, kind="ExternalOutput").ap()
    block_kernel(nc, *args, out)
    result = run_bass_kernel_spmd(nc, [{"in_" + n: a for n, a in arrays.items()}], core_ids=[0])
    return result.results[0]["out"]
```
